# Optimizing a Trainium2 kernel written in Bass

```python
import numpy as np
import jax
import jax.numpy as jnp

def _softmax(x, axis=-1):
    return jax.nn.softmax(x, axis=axis)
def _gelu(x):
    return jax.nn.gelu(x, approximate=True)
def _silu(x):
    return jax.nn.silu(x)
def _sigmoid(x):
    return jax.nn.sigmoid(x)
def _layernorm(x, axis=-1, eps=1e-5):
    m = jnp.mean(x, axis=axis, keepdims=True)
    v = jnp.var(x, axis=axis, keepdims=True)
    return (x - m) / jnp.sqrt(v + eps)
def _scatter_add(tgt, idx, src, axis=0):
    return tgt.at[idx].add(src)
def _segment_sum(src, seg, n):
    return jax.ops.segment_sum(src, seg, n)

kernel_name = 'mk_conv_preact_d2_conv_nhwc192_0cebe4'

def setup_inputs(seed: int = 0):
    np.random.seed(seed)
    _w = jnp.asarray
    def _rec_inputs():
        import jax
        import jax.numpy as jnp
        _gk = jax.random.key(seed)
        x = -0.0001476 + 0.9999 * jax.random.normal(jax.random.fold_in(_gk, 1), (64, 56, 56, 192), jnp.float32)
        return x
    x = _rec_inputs()
    def _L0_conv_setup():
        import jax, jax.numpy as jnp
        import numpy as np
        B, H, W, C = (64, 56, 56, 192)
        WS, SHIFT, NH = (7, 3, 6)
        HD = C // NH
        NWH, NWW = (H // WS, W // WS)
        NW = NWH * NWW
        L = WS * WS

        def _rel_index():
            coords = np.stack(np.meshgrid(np.arange(WS), np.arange(WS), indexing='ij')).reshape(2, -1)
            rel = (coords[:, :, None] - coords[:, None, :]).transpose(1, 2, 0)
            rel[..., 0] += WS - 1
            rel[..., 1] += WS - 1
            rel[..., 0] *= 2 * WS - 1
            return rel.sum(-1)

        def _attn_mask():
            img = np.zeros((H, W))
            cnt = 0
            for hs in (slice(0, -WS), slice(-WS, -SHIFT), slice(-SHIFT, None)):
                for ws_ in (slice(0, -WS), slice(-WS, -SHIFT), slice(-SHIFT, None)):
                    img[hs, ws_] = cnt
                    cnt += 1
            mw = img.reshape(NWH, WS, NWW, WS).transpose(0, 2, 1, 3).reshape(NW, L)
            diff = mw[:, None, :] - mw[:, :, None]
            return np.where(diff != 0, -100.0, 0.0).astype(np.float32)
        _REL_IDX = _rel_index()
        _MASK = _attn_mask()
        key = jax.random.key(seed)
        ks = jax.random.split(key, 4)
        return {'x': jax.random.normal(ks[0], (B, H, W, C), dtype=jnp.float32), 'qkv_w': jax.random.normal(ks[1], (C, 3 * C), dtype=jnp.float32) * 0.02, 'qkv_b': jnp.zeros((3 * C,), dtype=jnp.float32), 'proj_w': jax.random.normal(ks[2], (C, C), dtype=jnp.float32) * 0.02, 'proj_b': jnp.zeros((C,), dtype=jnp.float32), 'rel_table': jax.random.normal(ks[3], ((2 * WS - 1) ** 2, NH), dtype=jnp.float32) * 0.02}
    _L0_conv_all = _L0_conv_setup()
    _L0_conv_in = {k: v for k, v in _L0_conv_all.items() if k in ('qkv_w', 'qkv_b', 'proj_w', 'proj_b', 'rel_table', )}
    del _L0_conv_all

    def _L1_conv_setup():
        import jax, jax.numpy as jnp
        import numpy as np
        B, H, W, C = (32, 112, 112, 192)
        KH = KW = 3
        key = jax.random.key(seed)
        k1, k2 = jax.random.split(key)
        x = jax.random.normal(k1, (B, H, W, C), dtype=jnp.float32)
        w = jax.random.normal(k2, (KH, KW, 1, C), dtype=jnp.float32) * 0.1
        b = jnp.zeros((C,), dtype=jnp.float32)
        return {'x': x, 'w': w, 'b': b}
    _L1_conv_all = _L1_conv_setup()
    _L1_conv_in = {k: v for k, v in _L1_conv_all.items() if k in ('w', 'b', )}
    del _L1_conv_all

    return {
        "x": x,
        "L0_conv_qkv_w": _L0_conv_in["qkv_w"],
        "L0_conv_qkv_b": _L0_conv_in["qkv_b"],
        "L0_conv_proj_w": _L0_conv_in["proj_w"],
        "L0_conv_proj_b": _L0_conv_in["proj_b"],
        "L0_conv_rel_table": _L0_conv_in["rel_table"],
        "L1_conv_w": _L1_conv_in["w"],
        "L1_conv_b": _L1_conv_in["b"],
    }

def reference(x, L0_conv_qkv_w, L0_conv_qkv_b, L0_conv_proj_w, L0_conv_proj_b, L0_conv_rel_table, L1_conv_w, L1_conv_b):
    import jax
    import jax.numpy as jnp
    def _L0_conv_ref(x, qkv_w, qkv_b, proj_w, proj_b, rel_table):
        import jax, jax.numpy as jnp
        import numpy as np
        B, H, W, C = (64, 56, 56, 192)
        WS, SHIFT, NH = (7, 3, 6)
        HD = C // NH
        NWH, NWW = (H // WS, W // WS)
        NW = NWH * NWW
        L = WS * WS

        def _rel_index():
            coords = np.stack(np.meshgrid(np.arange(WS), np.arange(WS), indexing='ij')).reshape(2, -1)
            rel = (coords[:, :, None] - coords[:, None, :]).transpose(1, 2, 0)
            rel[..., 0] += WS - 1
            rel[..., 1] += WS - 1
            rel[..., 0] *= 2 * WS - 1
            return rel.sum(-1)

        def _attn_mask():
            img = np.zeros((H, W))
            cnt = 0
            for hs in (slice(0, -WS), slice(-WS, -SHIFT), slice(-SHIFT, None)):
                for ws_ in (slice(0, -WS), slice(-WS, -SHIFT), slice(-SHIFT, None)):
                    img[hs, ws_] = cnt
                    cnt += 1
            mw = img.reshape(NWH, WS, NWW, WS).transpose(0, 2, 1, 3).reshape(NW, L)
            diff = mw[:, None, :] - mw[:, :, None]
            return np.where(diff != 0, -100.0, 0.0).astype(np.float32)
        _REL_IDX = _rel_index()
        _MASK = _attn_mask()
        bias = jnp.transpose(rel_table[_REL_IDX], (2, 0, 1))
        mask = jnp.asarray(_MASK)
        xs = jnp.roll(x, (-SHIFT, -SHIFT), axis=(1, 2))
        xw = xs.reshape(B, NWH, WS, NWW, WS, C).transpose(0, 1, 3, 2, 4, 5).reshape(B, NW, L, C)
        qkv = (xw @ qkv_w + qkv_b).reshape(B, NW, L, 3, NH, HD)
        q = qkv[:, :, :, 0] * HD ** (-0.5)
        k = qkv[:, :, :, 1]
        v = qkv[:, :, :, 2]
        attn = jnp.einsum('bwihd,bwjhd->bwhij', q, k)
        attn = attn + bias[None, None] + mask[None, :, None]
        attn = jax.nn.softmax(attn, axis=-1)
        out = jnp.einsum('bwhij,bwjhd->bwihd', attn, v).reshape(B, NW, L, C)
        out = out @ proj_w + proj_b
        out = out.reshape(B, NWH, NWW, WS, WS, C).transpose(0, 1, 3, 2, 4, 5).reshape(B, H, W, C)
        return jnp.roll(out, (SHIFT, SHIFT), axis=(1, 2))

    def _L1_conv_ref(x, w, b):
        import jax, jax.numpy as jnp
        import numpy as np
        B, H, W, C = (32, 112, 112, 192)
        KH = KW = 3
        out = jax.lax.conv_general_dilated(x, w, window_strides=(1, 1), padding='SAME', rhs_dilation=(1, 1), dimension_numbers=('NHWC', 'HWIO', 'NHWC'), feature_group_count=C)
        return out + b

    def _gn(v, G=32, eps=1e-5):
        B_, H_, W_, C_ = v.shape
        g = v.reshape(B_, H_, W_, G, C_ // G)
        m = jnp.mean(g, axis=(1, 2, 4), keepdims=True)
        s = jnp.var(g, axis=(1, 2, 4), keepdims=True)
        return ((g - m) / jnp.sqrt(s + eps)).reshape(v.shape)

    def _ln_c(v, eps=1e-6):
        m = jnp.mean(v, axis=-1, keepdims=True)
        s = jnp.var(v, axis=-1, keepdims=True)
        return (v - m) / jnp.sqrt(s + eps)

    def _ln_t(v, eps=1e-5):
        m = jnp.mean(v, axis=-1, keepdims=True)
        s = jnp.var(v, axis=-1, keepdims=True)
        return (v - m) / jnp.sqrt(s + eps)

    def _to_tokens(v):
        B_, H_, W_, C_ = v.shape
        return v.reshape(B_, H_ * W_, C_)
    def _from_tokens(t, like):
        return t.reshape(like.shape)

    x = x + _L0_conv_ref(_gn(x), L0_conv_qkv_w, L0_conv_qkv_b, L0_conv_proj_w, L0_conv_proj_b, L0_conv_rel_table)
    x = x + _L1_conv_ref(_gn(x), L1_conv_w, L1_conv_b)
    return x


_drawn_inputs = setup_inputs


def setup_inputs(seed=0):
    import zlib

    import numpy as np

    out = dict(_drawn_inputs(seed))
    spreads = {'L0_conv_qkv_b': (0.0, 0.287), 'L0_conv_proj_b': (0.0, 0.1), 'L1_conv_b': (0.0, 0.1)}
    factors = {'L0_conv_qkv_w': 4.642, 'L0_conv_rel_table': 29.909}
    for name, (base, spread) in spreads.items():
        noise = np.random.default_rng([zlib.crc32(name.encode()), seed]).standard_normal(out[name].shape)
        drawn = base * np.exp(spread * noise) if base else spread * noise
        out[name] = jnp.asarray(drawn.astype(out[name].dtype))
    for name, factor in factors.items():
        out[name] = (out[name] * factor).astype(out[name].dtype)
    return out
```

```python
import concourse.bass as bass
from concourse import mybir
from contextlib import ExitStack

IMAGES, HH, WW, CH = 64, 56, 56, 192
WS, SHIFT, HEADS = 7, 3, 6
HD = CH // HEADS
STRIPS = HH // WS
WIN = WW // WS
L = WS * WS
TOK = WIN * L
PIX = HH * WW
ALL = IMAGES * STRIPS
MAIN = 128
TAIL = CH - MAIN
WP = 64
WN = 50
NX = 3
GROUP = CH // 32
EPS = 1e-5
LAG_STATS, LAG_NORM, LAG_SCORES, LAG_OUT, LAG_PROJ, LAG_CONV = -9, -1, 1, 2, 3, 11
XW = 60
MAIN_ROWS = 59
HALF = 28
TAIL_ROWS = 31
TAIL_STEP = 4
POOL_TAPS = (6, 7, 8)
SCALE = float(HD) ** -0.5


def swin_conv_kernel(nc, x, wqkv, vecs, bias, mask, gavg, convw, ident_d, y_main, y_tail):
    f32, f32r = mybir.dt.float32, mybir.dt.float32r
    ALU, ACT, AX = mybir.AluOpType, mybir.ActivationFunctionType, mybir.AxisListType
    ctx = ExitStack()
    with ctx:
        def sb(name, shape, dt=f32):
            return ctx.enter_context(nc.sbuf_tensor(name, shape, dt))

        def sem(name):
            return ctx.enter_context(nc.semaphore(name))

        XS = PIX
        Xm = sb("Xm", [128, NX * XS])
        Xt = sb("Xt", [TAIL, NX * XS])
        x1m = sb("x1m", [128, 2 * MAIN_ROWS * XW])
        x1t = sb("x1t", [128, 2 * TAIL_ROWS * XW])
        XN = WIN * WP
        nm = sb("nm", [128, TOK])
        nt = sb("nt", [TAIL, TOK])
        xmh = sb("xmh", [128, XN], f32r)
        xml = sb("xml", [128, XN], f32r)
        xts = sb("xts", [128, XN], f32r)
        qm = sb("qm", [128, 2, TOK])
        km = sb("km", [128, 2, TOK])
        qt = sb("qt", [TAIL, 2, TOK])
        kt = sb("kt", [TAIL, 2, TOK])
        V = sb("V", [128, 2, WIN, 3, 64])
        sT = sb("sT", [128, 2, 2, HEADS * L])
        mx = sb("mx", [128, 2, 2 * HEADS])
        sm = sb("sm", [128, 2, 2 * HEADS])
        rc = sb("rc", [128, 2, 2 * HEADS])
        P = sb("P", [128, 2, 4 * HEADS * 64])
        PT = sb("PT", [128, 2, 3 * 2 * L])
        omh = sb("omh", [128, TOK], f32r)
        oml = sb("oml", [128, TOK], f32r)
        ots = sb("ots", [128, TOK], f32r)
        ym = sb("ym", [128, 2, 8 * WW])
        yt = sb("yt", [128, 2, TAIL_STEP * WW])
        prod = sb("prod", [128, 3, TAIL_STEP * WW])
        NW = 3 * CH
        NWP = NW + CH + TAIL
        wf = P[:, :, :].rearrange("p a b -> p (a b)")[:, 0:2 * NWP].rearrange("p (t c) -> p t c", t=2)
        wmh = sb("wmh", [128, NW + CH + TAIL], f32r)
        wml = sb("wml", [128, NW + CH + TAIL], f32r)
        wth = sb("wth", [128, NW + CH + TAIL], f32r)
        wtl = sb("wtl", [128, NW + CH + TAIL], f32r)
        vec = sb("vec", [128, 12])
        b0 = sb("b0", [128, HEADS, L])
        mk = sb("mk", [128, 2, 2, L])
        zeros = sb("zeros", [128, 2 * MAIN_ROWS])
        BM = sb("BM", [128, 2, 2, HEADS * L])
        G = sb("G", [128, 3, 256])
        cw = sb("cw", [128, 2, 9])
        tick = sb("tick", [128, 3])
        ident = sb("ident", [128, 128])
        half = sb("half", [128, 2])
        bp = sb("bp", [128, 2])
        bq = sb("bq", [128, 2])
        bpc = sb("bpc", [128, 2])
        wsum = sb("wsum", [128, 2])
        st1 = sb("st1", [128, 2, STRIPS, 6])
        st2 = sb("st2", [128, 2, STRIPS + 1, 6])
        mv = sb("mv", [128, 2, 2, 2])
        dv = sb("dv", [128, 2, 2])
        t2 = sb("t2", [128, 2, 2])
        gme = sb("gme", [128, 2, 2])
        gve = sb("gve", [128, 2, 2])
        rs = sb("rs", [128, 2, 2])
        nb1 = sb("nb1", [128, 2])
        mfill = sb("mfill", [128, 2])
        ms = sb("ms", [128, 2])
        mw = sb("mw", [128, 2])
        weff = sb("weff", [128, 2, 9])
        b2 = sb("b2", [128, 2])

        def bank(name, n=1):
            return ctx.enter_context(nc.psum_tensor(name, [128, n, 512], f32))

        psS, psT, psO, psR = bank("psS", 4), bank("psT"), bank("psO", 2), bank("psR")
        ST0 = 400

        x_loaded = sem("x_loaded")
        consts = sem("consts")
        ticked = sem("ticked")
        setup_dve = sem("setup_dve")
        setup_pe = sem("setup_pe")
        wsplit = sem("wsplit")
        x_stats = sem("x_stats")
        normed = sem("normed")
        high = sem("high")
        low_m = sem("low_m")
        low_t = sem("low_t")
        qk_done = sem("qk_done")
        v_done = sem("v_done")
        qk_out = sem("qk_out")
        v_out = sem("v_out")
        s_done = sem("s_done")
        biased = sem("biased")
        maxed = sem("maxed")
        centred = sem("centred")
        exped = sem("exped")
        summed = sem("summed")
        recip = sem("recip")
        probs = sem("probs")
        pt_done = sem("pt_done")
        pt_out = sem("pt_out")
        av_done = sem("av_done")
        o_high = sem("o_high")
        o_low = sem("o_low")
        proj_done = sem("proj_done")
        resid = sem("resid")
        x1_stats = sem("x1_stats")
        gn = [sem("gn1"), sem("gn2")]
        gn_pe = [sem("gn1_pe"), sem("gn2_pe")]
        gn_pow = [sem("gn1_pow"), sem("gn2_pow")]
        fixed = sem("fixed")
        conv_m = sem("conv_m")
        TD = 9 - len(POOL_TAPS)
        conv_t = sem("conv_t")
        prods = sem("prods")
        conv_p = sem("conv_p")
        stored = [sem("stored0"), sem("stored1")]
        GN_DVE = [9, 15]
        FIX = 12

        def upto(per, strip, part, last=ALL - 1):
            if isinstance(strip, int):
                if strip < 0:
                    return 0
                if strip > last:
                    strip, part = last, per
            return strip * per + part

        def settle(eng):
            eng.reg_alu(scratch[eng], scratch[eng], 0, ALU.add)

        scratch = {}

        def xcol(n, r, width):
            off = (n % NX) * XS + r * TOK
            return off, width

        def tok(v):
            return v.rearrange("p (w t) -> p w t", t=WP)[:, :, 0:L]

        def wt(v):
            return v.rearrange("p (w t) -> p w t", t=L)

        def Xv(buf, parts, n, r, width):
            off, w = xcol(n, r, width)
            return buf[0:parts, bass.ds(off, w)]

        def grid(buf, p0, p1, base, rows, r0, nr, c0, ncol):
            v = buf[p0:p1, bass.ds(base, rows * XW)]
            return v.rearrange("p (r c) -> p r c", c=XW)[:, r0:r0 + nr, c0:c0 + ncol]

        def x1main(n, r0, nr, c0, ncol):
            return grid(x1m, 0, 128, (n % 2) * (MAIN_ROWS * XW), MAIN_ROWS, r0, nr, c0, ncol)

        def x1tail(n, p0, p1, r0, nr, c0, ncol):
            return grid(x1t, p0, p1, (n % 2) * (TAIL_ROWS * XW), TAIL_ROWS, r0, nr, c0, ncol)

        def stage(t_img, r, lag):
            k = r - lag
            return t_img + k // STRIPS, k % STRIPS

        def live(n, r):
            return not isinstance(n, int) or (0 <= n < IMAGES)

        def closes(n, r):
            return r == STRIPS - 1 and live(n, r)

        def gidx(n, r):
            return n * STRIPS + r

        def schedule(eng, slot):
            scratch[eng] = eng.alloc_register("settle")
            eng.reg_mov(scratch[eng], 0)
            for n in (-2, -1, 0, 1):
                for r in range(STRIPS):
                    slot(n, r)
            with eng.Fori(2, IMAGES - 2, 1) as n:
                for r in range(STRIPS):
                    slot(n, r)
            for n in range(IMAGES - 2, IMAGES + 2):
                for r in range(STRIPS):
                    slot(n, r)

        vq, vk, vv, vpj, vcv = (vec[:, i:i + 2] for i in (0, 2, 4, 6, 8))
        SETUP = 5
        block = ctx.enter_context(nc.Block())

        @block.sync
        def _(sp):
            for dst, src in ((wf[:, 0, :], wqkv[0:128, :]), (wf[0:64, 1, :], wqkv[128:192, :]),
                             (wf[64:128, 1, :], wqkv[128:192, :]), (vec[:, :], vecs),
                             (b0[:, :, :], bias), (mk[:, :, :, :], mask), (G[:, :, :], gavg), (cw[:, :, :], convw),
                             (ident[:, :], ident_d)):
                sp.dma_start(dst, src).then_inc(consts, 16)

            def slot(n, r):
                m = n + 2
                if r == 3 and live(m, 0):
                    sp.wait_ge(x_loaded, upto(32, m - 1, 32, IMAGES - 1))
                    sp.wait_ge(resid, upto(4, gidx(m - NX, STRIPS - 1), 4))
                    load(m)
                cn, cr = stage(n, r, LAG_CONV)
                if live(cn, cr):
                    g = gidx(cn, cr)
                    b = cr % 2
                    rows = WS + (cr == STRIPS - 1)
                    sp.wait_ge(conv_m, upto(9, g, 9))
                    sp.dma_start(y_main[cn, :, cr * TOK:cr * TOK + rows * WW],
                                 ym[:, b, 0:rows * WW]).then_inc(stored[b], 16)
                    tr = TAIL_STEP if cr < STRIPS - 1 else 1
                    sp.wait_ge(conv_p, upto(3, g, 3))
                    sp.dma_start(y_tail[cn, :, cr * TAIL_STEP * WW:(cr * TAIL_STEP + tr) * WW],
                                 yt[:, b, 0:tr * WW]).then_inc(stored[b], 16)

            def load(m):
                sp.dma_start(Xm[:, bass.ds((m % NX) * XS, PIX)], x[m, 0:128, :]).then_inc(x_loaded, 16)
                sp.dma_start(Xt[:, bass.ds((m % NX) * XS, PIX)], x[m, 128:192, :]).then_inc(x_loaded, 16)

            schedule(sp, slot)
            for b in range(2):
                sp.wait_ge(stored[b], 32 * (ALL // 2))

        @block.tensor
        def _(pe):
            mm = nc.tensor.matmul

            def split5(out, wc, rhs_m, rhs_ml, rhs_t, w_first):
                terms = ((wmh[:, wc], rhs_m), (wml[:, wc], rhs_m), (wmh[:, wc], rhs_ml),
                         (wth[:, wc], rhs_t), (wtl[0:64, wc], rhs_t[0:64]))
                for i, (w, v) in enumerate(terms):
                    a, b = (w, v) if w_first else (v, w)
                    last = mm(out, a, b, start=(i == 0), stop=(i == 4))
                return last

            pe.wait_ge(consts, 16 * 9)
            pe.wait_ge(setup_dve, 1)
            for tl, c0 in ((0, NW), (1, NW + 128)):
                mm(psT[:, 0, ST0 + tl:ST0 + tl + 1], wf[:, 0, c0:c0 + 128], vv[:, 0:1], start=True, stop=False)
                last = mm(psT[:, 0, ST0 + tl:ST0 + tl + 1], wf[0:64, 1, c0:c0 + 128], vv[0:64, 1:2], start=False, stop=True)
            last.then_inc(setup_pe, 1)
            pe.wait_ge(wsplit, 4)

            def scores(n, r, h):
                g = gidx(n, r)
                if h == 0:
                    pe.wait_ge(qk_out, upto(4, g, 4))
                    pe.wait_ge(biased, upto(4, g - 1, 4))
                else:
                    pe.wait_ge(biased, upto(4, g, 2))
                for pair in (2 * h, 2 * h + 1):
                    for w in range(2):
                        c0 = (pair * 2 + w) * L
                        for hd in range(HEADS):
                            q, k, p = (qm, km, 32 * hd) if hd < 4 else (qt, kt, 32 * (hd - 4))
                            col = (hd // 4 * 4 + pair) * L
                            last = mm(psS[64 * w:64 * w + L, hd % 4, col:col + L],
                                      q[p:p + 32, r % 2, c0:c0 + L],
                                      k[p:p + 32, r % 2, c0:c0 + L],
                                      start=True, stop=True)
                last.then_inc(s_done, 1)

            def transpose_probs(n, r, pair):
                g = gidx(n, r)
                pe.wait_ge(probs, upto(2, g, pair // 2 + 1))
                pe.wait_ge(pt_out, upto(4, g, pair)) if pair else pe.wait_ge(pt_out, upto(4, g - 1, 4))
                for q in range(3):
                    c0 = (pair * HEADS + 2 * q) * 64
                    last = nc.tensor.transpose(psT[:, 0, q * 128:q * 128 + 128],
                                               P[:, r % 2, c0:c0 + 128], ident[:, :])
                last.then_inc(pt_done, 1)

            def attend(n, r, pair):
                g = gidx(n, r)
                pe.wait_ge(pt_out, upto(4, g, pair + 1))
                if pair == 0:
                    pe.wait_ge(v_out, upto(8, g, 8))
                    pe.wait_ge(resid, upto(4, g - 1, 4))
                for w in range(2):
                    wi = pair * 2 + w
                    for q in range(3):
                        out = psO[64 * (q % 2):64 * (q % 2) + 64, q // 2, wi * L:wi * L + L]
                        p0 = (q * 2 + w) * L
                        last = mm(out, V[:, r % 2, wi, q, :], PT[:, pair % 2, p0:p0 + L],
                                  start=True, stop=True)
                last.then_inc(av_done, 1)

            def qk(n, r, j):
                g = gidx(n, r)
                if j == 0:
                    pe.wait_ge(high, upto(2, g, 2))
                    pe.wait_ge(low_m, upto(1, g, 1))
                    pe.wait_ge(low_t, upto(1, g, 1))
                    pe.wait_ge(v_out, upto(8, g - 1, 8))
                else:
                    pe.wait_ge(qk_out, upto(4, g, j))
                split5(psR[:, 0, 0:WIN * WN], slice(128 * j, 128 * j + 128), even(xmh),
                       even(xml), even(xts), True).then_inc(qk_done, 1)

            def even(buf):
                return buf[:, :].rearrange("k (w t) -> k w t", t=WP)[:, :, 0:WN]

            def windows(buf, p):
                return buf[:, p * 2 * WP:(p + 1) * 2 * WP]

            def values(n, r, i):
                g = gidx(n, r)
                if i:
                    pe.wait_ge(v_out, upto(8, g, 4))
                else:
                    pe.wait_ge(qk_out, upto(4, g, 4))
                for pr in range(2):
                    p = 2 * i + pr
                    last = split5(psR[:, 0, pr * CH:pr * CH + CH], slice(2 * CH, 3 * CH),
                                  windows(xmh, p), windows(xml, p), windows(xts, p), False)
                last.then_inc(v_done, 1)

            def project(n, r):
                g = gidx(n, r)
                pe.wait_ge(o_high, upto(2, g, 2))
                pe.wait_ge(o_low, upto(2, g, 2))
                for tl in range(2):
                    c0 = NW + 128 * tl
                    split5(psO[:, tl, 0:TOK], slice(c0, c0 + 128), omh[:, :], oml[:, :], ots[:, :],
                           True).then_inc(proj_done, 1)

            def averages(k, n, i):
                src = t2[:, k, :] if i else mv[:, k, :, 0]
                pe.wait_ge(gn[k], upto(GN_DVE[k], n, (3 + k, 7 + k)[i], IMAGES - 1))
                for tl in range(2):
                    c0 = ST0 + 8 * k + 4 * i + tl
                    o = psS[:, 0, c0:c0 + 1]
                    mm(o, G[:, 0, 128 * tl:128 * tl + 128], src[:, 0:1], start=True, stop=False)
                    last = mm(o, G[:, 1 + k, 128 * tl:128 * tl + 128], src[:, 1:2], start=False, stop=True)
                last.then_inc(gn_pe[k], 1)

            def slot(n, r):
                s, o, b, p = stage(n, r, LAG_SCORES), stage(n, r, LAG_OUT), (n, r), stage(n, r, LAG_PROJ)
                a1, a2 = stage(n, r, LAG_STATS + 1), stage(n, r, LAG_STATS + 2)
                p1 = stage(n, r, LAG_PROJ + 1)
                if live(*o):
                    transpose_probs(*o, 0)
                if live(*p):
                    project(*p)
                if closes(*p1):
                    averages(1, p1[0], 1)
                if closes(*a1):
                    averages(0, a1[0], 0)
                if closes(*a2):
                    pe.wait_ge(gn[0], upto(GN_DVE[0], a2[0], 8, IMAGES - 1))
                if live(*s):
                    scores(*s, 0)
                for pair in range(4):
                    if live(*b):
                        if pair < 3:
                            qk(*b, pair)
                        else:
                            values(*b, 0)
                    if live(*o):
                        attend(*o, pair)
                        if pair < 3:
                            transpose_probs(*o, pair + 1)
                    if pair == 1:
                        if closes(*p1):
                            pe.wait_ge(gn[1], upto(GN_DVE[1], p1[0], 9, IMAGES - 1))
                        if closes(*a1):
                            averages(0, a1[0], 1)
                        if closes(*p):
                            averages(1, p[0], 0)
                        if live(*s):
                            scores(*s, 1)
                if live(*b):
                    values(*b, 1)

            schedule(pe, slot)

        @block.scalar
        def _(act):
            A = nc.scalar.activation
            act.wait_ge(setup_dve, SETUP)

            def normalise(n, r):
                g = gidx(n, r)
                act.wait_ge(gn[0], upto(GN_DVE[0], n, GN_DVE[0], IMAGES - 1))
                act.wait_ge(low_m, upto(1, g - 1, 1))
                act.wait_ge(low_t, upto(1, g - 1, 1))
                act.wait_ge(x_loaded, upto(32, n, 32, IMAGES - 1))
                if not isinstance(n, int):
                    settle(act)
                A(wt(nm[:, :]), wt(Xv(Xm, 128, n, r, TOK)), ACT.Identity, scale=rs[:, 0, 0:1],
                  bias=nb1[:, 0:1]).then_inc(normed, 1)
                A(wt(nt[:, :]), wt(Xv(Xt, TAIL, n, r, TOK)), ACT.Identity, scale=rs[0:TAIL, 0, 1:2],
                  bias=nb1[0:TAIL, 1:2]).then_inc(normed, 1)

            def split(n, r):
                g = gidx(n, r)
                act.wait_ge(normed, upto(2, g, 1))
                act.wait_ge(v_done, upto(2, g - 1, 2))
                A(tok(xmh[:, :]), wt(nm[:, :]), ACT.Copy).then_inc(high, 1)
                act.wait_ge(normed, upto(2, g, 2))
                A(tok(xts[0:64, :]), wt(nt[:, :]), ACT.Copy).then_inc(high, 1)

            def win50(v):
                return v.rearrange("p (w t) -> p w t", t=WN)[:, :, 0:L]

            def evacuate_qk(n, r, j):
                g = gidx(n, r)
                act.wait_ge(qk_done, upto(3, g, j + 1))
                if j == 0:
                    act.wait_ge(s_done, upto(2, g - 2, 2))
                if j == 0:
                    A(wt(qm[:, r % 2, :]), win50(psR[:, 0, 0:WIN * WN]), ACT.Identity, scale=SCALE,
                      bias=bq[:, 0:1]).then_inc(qk_out, 1)
                elif j == 1:
                    A(wt(km[:, r % 2, :]), win50(psR[:, 0, 0:WIN * WN]), ACT.Identity, bias=vk[:, 0:1]).then_inc(qk_out, 1)
                else:
                    A(wt(qt[:, r % 2, :]), win50(psR[0:64, 0, 0:WIN * WN]), ACT.Identity, scale=SCALE,
                      bias=bq[0:64, 1:2]).then_inc(qk_out, 1)
                    A(wt(kt[:, r % 2, :]), win50(psR[64:128, 0, 0:WIN * WN]), ACT.Identity,
                      bias=vec[64:128, 3:4]).then_inc(qk_out, 1)

            def evacuate_v(n, r, i):
                g = gidx(n, r)
                act.wait_ge(v_done, upto(2, g, i + 1))
                if i == 0:
                    act.wait_ge(av_done, upto(4, g - 2, 4))
                for w in range(2):
                    for odd in range(2):
                        src = psR[64 * w:64 * w + 64, 0, 0:2 * CH].rearrange(
                            "p (a q e d) -> p a q e d", a=2, q=3, e=2)[:, :, :, odd, :]
                        dst = V[64 * odd:64 * odd + 64, r % 2, 4 * i + w:4 * i + w + 3:2, :,
                                32 * odd:32 * odd + 32]
                        A(dst, src, ACT.Copy).then_inc(v_out, 1)

            def exponentials(n, r, h):
                g = gidx(n, r)
                act.wait_ge(centred, upto(2, g, h + 1))
                act.wait_ge(pt_done, upto(4, g - 2, 2 * h + 2))
                dst = P[:, r % 2, h * 2 * HEADS * 64:(h + 1) * 2 * HEADS * 64].rearrange(
                    "p (s j) -> p s j", j=64)[:, :, 0:L]
                A(dst, sT[:, h, :, :].rearrange("p a (s j) -> p (a s) j", j=L),
                  ACT.Exp).then_inc(exped, 1)

            def evacuate_pt(n, r, pair):
                g = gidx(n, r)
                act.wait_ge(pt_done, upto(4, g, pair + 1))
                act.wait_ge(av_done, upto(4, g, pair - 1)) if pair > 1 else act.wait_ge(av_done, upto(4, g - 1, pair + 3))
                src = psT[:, 0, 0:384].rearrange("p (s i) -> p s i", i=64)[:, :, 0:L]
                A(PT[:, pair % 2, :].rearrange("p (s i) -> p s i", i=L), src,
                  ACT.Copy).then_inc(pt_out, 1)

            def evacuate_o(n, r):
                g = gidx(n, r)
                act.wait_ge(av_done, upto(4, g, 4))
                act.wait_ge(proj_done, upto(2, g - 1, 2))
                A(omh[:, :], psO[:, 0, 0:TOK], ACT.Copy).then_inc(o_high, 1)
                A(ots[0:64, :], psO[0:64, 1, 0:TOK], ACT.Copy).then_inc(o_high, 1)

            def products(n, r):
                g = gidx(n, r)
                rows = TAIL_STEP if r < STRIPS - 1 else 1
                act.wait_ge(fixed, upto(FIX, n, FIX, IMAGES - 1))
                act.wait_ge(conv_p, upto(3, g - 1, 3))
                if not isinstance(n, int):
                    settle(act)
                for i, tap in enumerate(POOL_TAPS):
                    dy, dx = tap // 3, tap % 3
                    A(prod[:, i, 0:rows * WW].rearrange("p (a b) -> p a b", b=WW),
                      x1tail(n, 0, 128, TAIL_STEP * r + dy, rows, dx, WW), ACT.Copy,
                      scale=weff[:, 1, tap:tap + 1]).then_inc(prods, 1)

            def slot(n, r):
                s, o, b, c = stage(n, r, LAG_SCORES), stage(n, r, LAG_OUT), (n, r), stage(n, r, LAG_CONV)
                m = stage(n, r, LAG_NORM)
                if live(*b):
                    split(*b)
                for pair in range(4):
                    if live(*o):
                        evacuate_pt(*o, pair)
                    if live(*b) and pair < 3:
                        evacuate_qk(*b, pair)
                    if live(*s) and pair in (0, 2):
                        exponentials(*s, pair // 2)
                if live(*b):
                    evacuate_v(*b, 0)
                if live(*o):
                    evacuate_o(*o)
                if live(*m):
                    normalise(*m)
                if live(*b):
                    evacuate_v(*b, 1)
                if live(*c):
                    products(*c)

            schedule(act, slot)

        @block.gpsimd
        def _(pool):
            TT = nc.gpsimd.tensor_tensor
            nc.gpsimd.memset(half[:, :], -0.5).then_inc(wsplit, 1)
            pool.wait_ge(setup_dve, SETUP)
            pool.wait_ge(wsplit, 4)

            def per_head(v):
                return v.unsqueeze(2).to_broadcast([128, 2 * HEADS, L])

            def centre(n, r, h):
                g = gidx(n, r)
                pool.wait_ge(maxed, upto(2, g, h + 1))
                v = sT[:, h, :, :].rearrange("p a (s j) -> p (a s) j", j=L)
                TT(v, v, per_head(mx[:, h, :]), ALU.subtract).then_inc(centred, 1)

            def normalise(n, r, h):
                g = gidx(n, r)
                pool.wait_ge(recip, upto(2, g, h + 1))
                v = P[:, r % 2, h * 2 * HEADS * 64:(h + 1) * 2 * HEADS * 64].rearrange(
                    "p (s j) -> p s j", j=64)[:, :, 0:L]
                TT(v, v, per_head(rc[:, h, :]), ALU.mult).then_inc(probs, 1)

            def low(n, r):
                g = gidx(n, r)
                pool.wait_ge(high, upto(2, g, 1))
                pool.wait_ge(v_done, upto(2, g - 1, 2))
                TT(tok(xml[:, :]), wt(nm[:, :]), tok(xmh[:, :].bitcast(f32)), ALU.subtract).then_inc(low_m, 1)

            def add_products(n, r):
                g = gidx(n, r)
                rows = TAIL_STEP if r < STRIPS - 1 else 1
                acc = yt[:, r % 2, 0:rows * WW]
                pool.wait_ge(conv_t, upto(TD, g, TD))
                for i in range(3):
                    pool.wait_ge(prods, upto(3, g, i + 1))
                    if i:
                        pool.wait_ge(conv_p, upto(3, g, i))
                    TT(acc, acc, prod[:, i, 0:rows * WW], ALU.add).then_inc(conv_p, 1)

            def power(k, n):
                pool.wait_ge(gn[k], upto(GN_DVE[k], n, 8 + k, IMAGES - 1))
                if k == 0:
                    pool.wait_ge(normed, upto(2, gidx(n - 1, STRIPS - 1), 2))
                TT(rs[:, k, :], gve[:, k, :], half[:, :], ALU.pow).then_inc(gn_pow[k], 1)

            def slot(n, r):
                s, b, c = stage(n, r, LAG_SCORES), (n, r), stage(n, r, LAG_CONV)
                a1, p1 = stage(n, r, LAG_STATS + 1), stage(n, r, LAG_PROJ + 1)
                if live(*b):
                    low(*b)
                if live(*s):
                    centre(*s, 0)
                if closes(*p1):
                    power(1, p1[0])
                if live(*s):
                    normalise(*s, 0)
                    centre(*s, 1)
                if closes(*a1):
                    power(0, a1[0])
                if live(*s):
                    normalise(*s, 1)
                if live(*c):
                    add_products(*c)

            schedule(pool, slot)

        @block.vector
        def _(dve):
            v_ = nc.vector
            for ps in (psS, psT, psO, psR):
                last = v_.memset(ps[:, :, :], 0.0)
            last.then_inc(setup_dve, 1)
            for buf in (x1m, x1t):
                v_.memset(buf[:, :], 0.0)
            v_.memset(V[:, :, :, :, :], 0.0)
            for buf in (st1, st2):
                v_.memset(buf[:, :, :, :], 0.0)
            for buf in (mv,):
                v_.memset(buf[:, :, :, :], 0.0)
            v_.memset(zeros[:, :], 0.0)
            for buf in (xmh, xml, xts):
                v_.memset(buf[:, :].bitcast(f32), 0.0)
            v_.memset(t2[:, :, :], 0.0).then_inc(setup_dve, 1)
            dve.wait_ge(setup_dve, 2)
            dve.wait_ge(consts, 16 * 9)
            for row in range(2):
                for col in range(2):
                    v_.tensor_tensor(BM[:, row, col, :].rearrange("p (h j) -> p h j", j=L), b0[:, :, :],
                                     mk[:, row, col, :].unsqueeze(1).to_broadcast([128, HEADS, L]), ALU.add)
            v_.tensor_copy(wmh[:, :], wf[:, 0, :])
            v_.tensor_copy(wth[:, :], wf[:, 1, :]).then_inc(setup_dve, 1)
            dve.wait_ge(setup_dve, 3)
            v_.tensor_tensor(wml[:, :], wf[:, 0, :], wmh[:, :].bitcast(f32), ALU.subtract).then_inc(wsplit, 1)
            v_.tensor_tensor(wtl[:, :], wf[:, 1, :], wth[:, :].bitcast(f32), ALU.subtract).then_inc(wsplit, 1)
            v_.tensor_scalar(bq[:, :], vq, SCALE, None, ALU.mult).then_inc(wsplit, 1)
            dve.wait_ge(setup_pe, 1)
            v_.tensor_tensor(bp[:, :], psT[:, 0, ST0:ST0 + 2], vpj, ALU.add)
            dve.wait_ge(wsplit, 4)
            v_.memset(P[:, :, :], 0.0)
            v_.reduce_sum(wsum[:, :], cw[:, :, :], AX.X).then_inc(setup_dve, 1)
            dve.wait_ge(setup_dve, 4)
            v_.tensor_tensor(bpc[:, :], bp[:, :], vcv, ALU.add).then_inc(setup_dve, 1)
            dve.wait_ge(setup_dve, 5)

            def x_statistics(n, r):
                g = gidx(n, r)
                if r == 0:
                    dve.wait_ge(ticked, upto(1, n - 1, 1, IMAGES - 1))
                    dve.wait_ge(x_loaded, upto(32, n, 32, IMAGES - 1))
                    dve.wait_ge(gn[0], upto(GN_DVE[0], n - 1, 3, IMAGES - 1))
                    v_.tensor_copy(tick[:, 2:3], zeros[:, 0:1]).then_inc(ticked, 1)
                v_.bn_stats(st1[:, 0, r, :], Xv(Xm, 128, n, r, TOK)).then_inc(x_stats, 1)
                v_.bn_stats(st1[0:64, 1, r, :], Xv(Xt, TAIL, n, r, TOK)).then_inc(x_stats, 1)

            def low_tail(n, r):
                g = gidx(n, r)
                dve.wait_ge(high, upto(2, g, 2))
                dve.wait_ge(v_done, upto(2, g - 1, 2))
                v_.tensor_tensor(tok(xts[64:128, :]), wt(nt[:, :]), tok(xts[0:64, :].bitcast(f32)),
                                 ALU.subtract).then_inc(low_t, 1)

            def bias_max(n, r, h):
                g = gidx(n, r)
                dve.wait_ge(s_done, upto(2, g, h + 1))
                dve.wait_ge(exped, upto(2, g - 1, h + 1))
                row = int(r == STRIPS - 1)
                table = BM[:, row, 0:1, :].to_broadcast([128, 2, HEADS * L]) if h == 0 else BM[:, row, :, :]
                for h0, h1, c0 in ((0, 4, 2 * h * L), (4, 6, (4 + 2 * h) * L)):
                    out, tab = (v[:, :, h0 * L:h1 * L].rearrange("p a (s j) -> p a s j", j=L)
                                for v in (sT[:, h, :, :], table))
                    src = psS[:, 0:h1 - h0, c0:c0 + 2 * L].rearrange("p s (a j) -> p a s j", a=2)
                    v_.tensor_tensor(out, src, tab, ALU.add).then_inc(biased, 1)
                dve.wait_ge(biased, upto(4, g, 2 * h + 2))
                dve.wait_ge(centred, upto(2, g - 1, h + 1))
                v_.reduce_max(mx[:, h, :], sT[:, h, :, :].rearrange("p a (s j) -> p (a s) j", j=L),
                              AX.X).then_inc(maxed, 1)

            def sums(n, r, h):
                g = gidx(n, r)
                dve.wait_ge(exped, upto(2, g, h + 1))
                src = P[:, r % 2, h * 2 * HEADS * 64:(h + 1) * 2 * HEADS * 64].rearrange(
                    "p (s j) -> p s j", j=64)[:, :, 0:L]
                v_.reduce_sum(sm[:, h, :], src, AX.X).then_inc(summed, 1)
                dve.wait_ge(summed, upto(2, g, h + 1))
                dve.wait_ge(probs, upto(2, g - 1, h + 1))
                v_.reciprocal(rc[:, h, :], sm[:, h, :]).then_inc(recip, 1)

            def o_lows(n, r):
                g = gidx(n, r)
                dve.wait_ge(o_high, upto(2, g, 1))
                dve.wait_ge(proj_done, upto(2, g - 1, 2))
                v_.tensor_tensor(oml[:, :], psO[:, 0, 0:TOK], omh[:, :].bitcast(f32), ALU.subtract).then_inc(o_low, 1)
                dve.wait_ge(o_high, upto(2, g, 2))
                v_.tensor_tensor(ots[64:128, :], psO[0:64, 1, 0:TOK], ots[0:64, :].bitcast(f32),
                                 ALU.subtract).then_inc(o_low, 1)

            def residual(n, r):
                g = gidx(n, r)
                dve.wait_ge(proj_done, upto(2, g, 1))
                if r == 0:
                    dve.wait_ge(conv_m, upto(9, gidx(n - 2, STRIPS - 1), 9))
                    dve.wait_ge(conv_t, upto(TD, gidx(n - 2, STRIPS - 1), TD))
                    dve.wait_ge(prods, upto(3, gidx(n - 2, STRIPS - 1), 3))
                r0 = WS * r
                cut = 53 - r0 if r == STRIPS - 1 else WS

                def win(v, a0, a1):
                    return v.rearrange("p (w a b) -> p w a b", a=WS, b=WS)[:, :, a0:a1, :]

                def rows(v):
                    return v.rearrange("p a (w b) -> p w a b", b=WS)

                def part(tile_, a0, a1):
                    if tile_ == 0:
                        dst = x1main(n, 1 + r0 + a0 + (a0 >= cut), a1 - a0, 4, WW)
                        src, xin = psO[:, 0, 0:TOK], Xv(Xm, 128, n, r, TOK)
                    else:
                        up = r < STRIPS // 2
                        row = 1 + r0 + a0 + (a0 >= cut) - (0 if up else HALF)
                        dst = x1tail(n, 0 if up else 64, 64 if up else 128, row, a1 - a0, 4, WW)
                        src, xin = psO[0:64, 1, 0:TOK], Xv(Xt, TAIL, n, r, TOK)
                    return v_.tensor_tensor(rows(dst), win(src, a0, a1), win(xin, a0, a1), ALU.add)

                for tl in range(2):
                    if tl:
                        dve.wait_ge(proj_done, upto(2, g, 2))
                    if cut < WS:
                        part(tl, 0, cut).then_inc(resid, 1)
                        part(tl, cut, WS).then_inc(resid, 1)
                    else:
                        part(tl, 0, WS).then_inc(resid, 2)

            def x1_statistics(n, r):
                r0 = WS * r
                pad = r == STRIPS - 1
                p0 = 0 if r < STRIPS // 2 else 64
                row = 1 + r0 - (HALF if p0 else 0)
                rr = r % (STRIPS // 2)
                for a0, a1, more in [(0, 4, 0), (4, WS, 1)] if pad else [(0, WS, 0)]:
                    i1 = v_.bn_stats(st2[:, 0, r + more, :], x1main(n, 1 + r0 + a0 + more, a1 - a0, 4, WW))
                for a0, a1, more in [(0, 4, 0), (4, WS, 1)] if rr == 3 else [(0, WS, 0)]:
                    i2 = v_.bn_stats(st2[p0:p0 + 64, 1, rr + more, :],
                                     x1tail(n, p0, p0 + 64, row + a0 + (more if pad else 0), a1 - a0, 4, WW))
                i1.then_inc(x1_stats, 1)
                i2.then_inc(x1_stats, 1)

            def norm_gather(k, n):
                dve.wait_ge(gn[k], upto(GN_DVE[k], n - 1, GN_DVE[k], IMAGES - 1))
                dve.wait_ge((x_stats, x1_stats)[k], upto(2, gidx(n, STRIPS - 1), 2))
                v_.tensor_copy(tick[:, k:k + 1], zeros[:, 0:1]).then_inc(gn[k], 1)
                if k == 0:
                    v_.bn_aggr(mv[:, 0, 0, :], st1[:, 0, :, :]).then_inc(gn[k], 1)
                    v_.bn_aggr(mv[0:64, 0, 1, :], st1[0:64, 1, :, :]).then_inc(gn[k], 1)
                else:
                    v_.bn_aggr(mv[:, 1, 0, :], st2[:, 0, 0:9, :]).then_inc(gn[k], 1)
                    v_.bn_aggr(mv[:, 1, 1, :], st2[:, 1, 0:5, :]).then_inc(gn[k], 1)
                    dve.wait_ge(gn[k], upto(GN_DVE[k], n, 3, IMAGES - 1))
                    v_.tensor_tensor(mv[:, 1, :, 0], mv[:, 1, :, 0], bp[:, :], ALU.add).then_inc(gn[k], 1)

            def norm_mean(k, n):
                c0 = ST0 + 8 * k
                dve.wait_ge(gn_pe[k], upto(2, n, 1, IMAGES - 1))
                v_.tensor_copy(gme[:, k, :], psS[:, 0, c0:c0 + 2]).then_inc(gn[k], 1)
                v_.tensor_tensor(dv[:, k, :], mv[:, k, :, 0], psS[:, 0, c0:c0 + 2], ALU.subtract).then_inc(gn[k], 1)
                dve.wait_ge(gn[k], upto(GN_DVE[k], n, 5 + k, IMAGES - 1))
                v_.tensor_tensor(t2[:, k, :], dv[:, k, :], dv[:, k, :], ALU.mult).then_inc(gn[k], 1)
                dve.wait_ge(gn[k], upto(GN_DVE[k], n, 6 + k, IMAGES - 1))
                v_.tensor_tensor(t2[:, k, :], t2[:, k, :], mv[:, k, :, 1], ALU.add).then_inc(gn[k], 1)

            def norm_var(k, n):
                c0 = ST0 + 8 * k
                dve.wait_ge(gn_pe[k], upto(2, n, 2, IMAGES - 1))
                v_.tensor_scalar(gve[:, k, :], psS[:, 0, c0 + 4:c0 + 6], EPS, None, ALU.add).then_inc(gn[k], 1)

            def norm_finish(k, n):
                dve.wait_ge(gn_pow[k], upto(1, n, 1, IMAGES - 1))
                if k == 0:
                    dve.wait_ge(normed, upto(2, gidx(n - 1, STRIPS - 1), 2))
                    v_.scalar_tensor_tensor(out=nb1[:, :], in0=gme[:, 0, :], scalar=-1.0,
                                                 in1=rs[:, 0, :], op0=ALU.mult, op1=ALU.mult).then_inc(gn[k], 1)
                else:
                    dve.wait_ge(conv_m, upto(9, gidx(n - 1, STRIPS - 1), 9))
                    dve.wait_ge(conv_t, upto(TD, gidx(n - 1, STRIPS - 1), TD))
                    dve.wait_ge(prods, upto(3, gidx(n - 1, STRIPS - 1), 3))
                    v_.tensor_tensor(mfill[:, :], gme[:, 1, :], bp[:, :], ALU.subtract).then_inc(gn[k], 1)
                    v_.tensor_tensor(weff[:, :, :], cw[:, :, :],
                                          rs[:, 1, :].unsqueeze(2).to_broadcast([128, 2, 9]), ALU.mult).then_inc(gn[k], 1)
                    dve.wait_ge(gn[k], upto(GN_DVE[k], n, 11, IMAGES - 1))
                    v_.tensor_scalar(weff[:, :, 4], weff[:, :, 4], 1.0, None, ALU.add).then_inc(gn[k], 1)
                    v_.tensor_tensor(ms[:, :], mfill[:, :], rs[:, 1, :], ALU.mult).then_inc(gn[k], 1)
                    dve.wait_ge(gn[k], upto(GN_DVE[k], n, 13, IMAGES - 1))
                    v_.tensor_tensor(mw[:, :], ms[:, :], wsum[:, :], ALU.mult).then_inc(gn[k], 1)
                    dve.wait_ge(gn[k], upto(GN_DVE[k], n, 14, IMAGES - 1))
                    v_.tensor_tensor(b2[:, :], bpc[:, :], mw[:, :], ALU.subtract).then_inc(gn[k], 1)

            def pads(n):
                def fill(dst, rows, cols, tl, p0=0):
                    z = zeros[p0:128, 0:rows * cols].rearrange("p (r c) -> p r c", c=cols)
                    v_.tensor_scalar(dst, z, mfill[p0:128, tl:tl + 1], None, ALU.add).then_inc(fixed, 1)

                dve.wait_ge(gn[1], upto(GN_DVE[1], n, 10, IMAGES - 1))
                R, C = MAIN_ROWS, TAIL_ROWS
                v_.tensor_copy(x1main(n, 1, R - 2, 1, 3), x1main(n, 1, R - 2, 57, 3)).then_inc(fixed, 1)
                v_.tensor_copy(x1tail(n, 0, 128, 1, C - 2, 1, 3), x1tail(n, 0, 128, 1, C - 2, 57, 3)).then_inc(fixed, 1)
                dve.wait_ge(fixed, upto(FIX, n, 2, IMAGES - 1))
                fill(x1main(n, 0, R, 0, XW)[:, :, 0:58:57], R, 2, 0)
                fill(x1tail(n, 0, 128, 0, C, 0, XW)[:, :, 0:58:57], C, 2, 1)
                dve.wait_ge(fixed, upto(FIX, n, 4, IMAGES - 1))
                fill(x1main(n, 54, 1, 0, XW), 1, XW, 0)
                fill(x1tail(n, 64, 128, 26, 1, 0, XW), 1, XW, 1, 64)
                dve.wait_ge(fixed, upto(FIX, n, 6, IMAGES - 1))
                v_.tensor_copy(x1main(n, 0, 1, 0, XW), x1main(n, R - 2, 1, 0, XW)).then_inc(fixed, 1)
                v_.tensor_copy(x1main(n, R - 1, 1, 0, XW), x1main(n, 1, 1, 0, XW)).then_inc(fixed, 1)
                v_.tensor_copy(x1tail(n, 0, 64, 0, 1, 0, XW), x1tail(n, 64, 128, 29, 1, 0, XW)).then_inc(fixed, 1)
                v_.tensor_copy(x1tail(n, 0, 64, 29, 1, 0, XW), x1tail(n, 64, 128, 1, 1, 0, XW)).then_inc(fixed, 1)
                v_.tensor_copy(x1tail(n, 64, 128, 0, 1, 0, XW), x1tail(n, 0, 64, 28, 1, 0, XW)).then_inc(fixed, 1)
                v_.tensor_copy(x1tail(n, 64, 128, 30, 1, 0, XW), x1tail(n, 0, 64, 1, 1, 0, XW)).then_inc(fixed, 1)

            MAIN_TAPS = [4, 0, 1, 2, 3, 5, 6, 7, 8]
            TAIL_TAPS = [tap for tap in MAIN_TAPS if tap not in POOL_TAPS]

            def convolve(n, r, i0, i1, tl):
                g = gidx(n, r)
                last = r == STRIPS - 1
                taps, done, per, acc = ((MAIN_TAPS, conv_m, 9, ym), (TAIL_TAPS, conv_t, TD, yt))[tl]
                rows = (WS + last) if tl == 0 else (1 if last else TAIL_STEP)
                step = WS if tl == 0 else TAIL_STEP
                y = acc[:, r % 2, 0:rows * WW].rearrange("p (a b) -> p a b", b=WW)
                for i in range(i0, i1):
                    tap = taps[i]
                    dy, dx = tap // 3, tap % 3
                    row = step * r + dy
                    v = x1main(n, row, rows, dx, WW) if tl == 0 else x1tail(n, 0, 128, row, rows, dx, WW)
                    if i == 0:
                        dve.wait_ge(gn[1], upto(GN_DVE[1], n, GN_DVE[1], IMAGES - 1))
                        dve.wait_ge(fixed, upto(FIX, n, FIX, IMAGES - 1))
                        if not isinstance(n, int) or g >= 2:
                            dve.wait_ge(stored[r % 2], g * 16 - 16 * (r % 2))
                        v_.tensor_scalar(y, v, weff[:, tl, tap:tap + 1], b2[:, tl:tl + 1],
                                         ALU.mult, ALU.add).then_inc(done, 1)
                    else:
                        dve.wait_ge(done, upto(per, g, i))
                        v_.scalar_tensor_tensor(out=y, in0=v, scalar=weff[:, tl, tap:tap + 1], in1=y,
                                                op0=ALU.mult, op1=ALU.add).then_inc(done, 1)

            def slot(n, r):
                s, o, b, p = stage(n, r, LAG_SCORES), stage(n, r, LAG_OUT), (n, r), stage(n, r, LAG_PROJ)
                a, a1, p1 = stage(n, r, LAG_STATS), stage(n, r, LAG_STATS + 1), stage(n, r, LAG_PROJ + 1)
                c = stage(n, r, LAG_CONV)

                def taps(i0, i1):
                    if live(*c):
                        for i in range(i0, i1):
                            convolve(*c, i, i + 1, 0)
                            if i < TD:
                                convolve(*c, i, i + 1, 1)

                if c[1]:
                    taps(0, 2)
                if live(*b):
                    low_tail(*b)
                if live(*p):
                    residual(*p)
                    dve.wait_ge(resid, upto(4, gidx(*p), 4))
                    if p[1] == 0:
                        dve.wait_ge(gn[1], upto(GN_DVE[1], p[0] - 1, 3, IMAGES - 1))
                if live(*s):
                    bias_max(*s, 0)
                if closes(*a1):
                    norm_mean(0, a1[0])
                if closes(*p1):
                    norm_var(1, p1[0])
                if live(*p):
                    x1_statistics(*p)
                if closes(*p):
                    norm_gather(1, p[0])
                if closes(*p1):
                    norm_finish(1, p1[0])
                    pads(p1[0])
                taps(2 if c[1] else 0, 4)
                if live(*s):
                    sums(*s, 0)
                    bias_max(*s, 1)
                if closes(*a1):
                    norm_var(0, a1[0])
                if closes(*p):
                    norm_mean(1, p[0])
                taps(4, 6)
                if live(*a):
                    x_statistics(*a)
                if closes(*a):
                    norm_gather(0, a[0])
                if live(*s):
                    sums(*s, 1)
                if closes(*a1):
                    norm_finish(0, a1[0])
                if live(*o):
                    o_lows(*o)
                taps(6, 9)

            schedule(dve, slot)


_SHAPES = [(IMAGES, 128, MAIN_ROWS * WW - 2 * WW), (IMAGES, 128, (TAIL_ROWS - 2) * WW)]


def kernel(x, L0_conv_qkv_w, L0_conv_qkv_b, L0_conv_proj_w, L0_conv_proj_b, L0_conv_rel_table,
           L1_conv_w, L1_conv_b):
    import numpy as _np
    import concourse.bacc as _bacc
    from concourse import mybir as _mybir
    from concourse.bass_utils import run_bass_kernel_spmd as _run

    f = _np.float32
    xs = _np.roll(_np.asarray(x), (-SHIFT, -SHIFT), axis=(1, 2))
    xw = _np.ascontiguousarray(xs.reshape(IMAGES, STRIPS, WS, WIN, WS, CH).transpose(0, 5, 1, 3, 2, 4)
                               ).reshape(IMAGES, CH, PIX)
    order = _np.concatenate([_np.arange(0, 128), CH + _np.arange(0, 128), _np.arange(128, CH),
                             CH + _np.arange(128, CH), 2 * CH + _np.arange(CH)])
    pw = _np.asarray(L0_conv_proj_w)
    wqkv = _np.concatenate([_np.asarray(L0_conv_qkv_w)[:, order], pw, pw[:, 128:]], axis=1)

    def tiles(v, twice=True):
        v = _np.asarray(v)
        return _np.stack([v[:128], _np.concatenate([v[128:], v[128:]])], axis=1)

    qb = _np.asarray(L0_conv_qkv_b)
    vecs = _np.concatenate([tiles(qb[:CH]), tiles(qb[CH:2 * CH]), tiles(qb[2 * CH:]),
                            tiles(L0_conv_proj_b), tiles(L1_conv_b), _np.zeros((128, 2), f)], axis=1)
    cw = _np.asarray(L1_conv_w).reshape(9, CH)
    convw = _np.stack([tiles(cw[t]) for t in range(9)], axis=2)
    co = _np.stack(_np.meshgrid(_np.arange(WS), _np.arange(WS), indexing="ij")).reshape(2, -1)
    rel = (co[:, :, None] - co[:, None, :]) + WS - 1
    idx = rel[0] * (2 * WS - 1) + rel[1]
    tab = _np.asarray(L0_conv_rel_table)[idx].transpose(0, 2, 1)
    bias = _np.zeros((128, HEADS, L), f)
    bias[0:L] = tab
    bias[64:64 + L] = tab
    late = (_np.arange(WS) >= WS - SHIFT).astype(int)
    mask = _np.zeros((128, 2, 2, L), f)
    for row in range(2):
        for col in range(2):
            for w in range(2):
                region = (late[:, None] * 2 * row + late[None, :] * (col and w)).reshape(-1)
                mask[64 * w:64 * w + L, row, col] = _np.where(region[:, None] != region[None, :], -100.0, 0.0)
    grp = _np.arange(CH) // GROUP
    same = (grp[:, None] == grp[None, :]).astype(f) / f(GROUP)
    same = _np.concatenate([same, same[:, 128:]], axis=1)
    gavg = _np.zeros((128, 3, 256), f)
    gavg[:, 0] = same[:128]
    gavg[:64, 1] = same[128:]
    gavg[:64, 2] = same[128:] / 2
    gavg[64:, 2] = same[128:] / 2
    ident = _np.eye(128, dtype=f)

    nc = _bacc.Bacc("TRN2", target_bir_lowering=False, num_devices=1)
    arrays, args = {}, []
    for name, a in (("x", xw), ("wqkv", wqkv), ("vecs", vecs), ("bias", bias), ("mask", mask),
                    ("gavg", gavg), ("convw", convw), ("ident", ident)):
        a = _np.ascontiguousarray(a)
        arrays[f"in_{name}"] = a
        args.append(nc.dram_tensor(f"in_{name}", a.shape, _mybir.dt.from_np(a.dtype), kind="ExternalInput").ap())
    for i, shape in enumerate(_SHAPES):
        args.append(nc.dram_tensor(f"out_{i}", shape, _mybir.dt.float32, kind="ExternalOutput").ap())
    swin_conv_kernel(nc, *args)
    r = _run(nc, [arrays], core_ids=[0])
    ym, yt = r.results[0]["out_0"], r.results[0]["out_1"]
    ym = _np.asarray(ym).reshape(IMAGES, 128, 57, WW)
    yt = _np.asarray(yt).reshape(IMAGES, 2, TAIL, 29, WW)
    main = _np.concatenate([ym[:, :, 54:], ym[:, :, :53]], axis=2)
    tail = _np.concatenate([yt[:, 1, :, 26:], yt[:, 0, :, :28], yt[:, 1, :, :25]], axis=2)
    y = _np.concatenate([main, tail], axis=1).transpose(0, 2, 3, 1)
    return _np.ascontiguousarray(y)
```

```python
import concourse.bass as bass
from concourse import mybir
from contextlib import ExitStack

IMAGES, HH, WW, CH = 64, 56, 56, 192
WS, SHIFT, HEADS = 7, 3, 6
HD = CH // HEADS
STRIPS = HH // WS
WIN = WW // WS
L = WS * WS
TOK = WIN * L
PIX = HH * WW
ALL = IMAGES * STRIPS
MAIN = 128
TAIL = CH - MAIN
WP = 64
WN = 50
NX = 3
GROUP = CH // 32
EPS = 1e-5
LAG_STATS, LAG_NORM, LAG_SCORES, LAG_OUT, LAG_PROJ, LAG_CONV, LAG_TAIL = -10, -1, 1, 2, 3, 11, 12
XW = 60
MAIN_ROWS = 59
HALF = 28
TAIL_ROWS = 31
TAIL_STEP = 4
TAPS = (4, 0, 1, 2, 3, 5, 6, 7, 8)
GROUPS = ((0, 3), (3, 5), (5, 8))
HOLD = (0, 1, 2, 3, 4, 5, 6, 3)
SCALE = float(HD) ** -0.5


def swin_conv_kernel(nc, x, wqkv, vecs, bias, mask, gavg, convw, ident_d, y_main, y_tail):
    f32, f32r = mybir.dt.float32, mybir.dt.float32r
    ALU, ACT, AX = mybir.AluOpType, mybir.ActivationFunctionType, mybir.AxisListType
    ctx = ExitStack()
    with ctx:
        def sb(name, shape, dt=f32):
            return ctx.enter_context(nc.sbuf_tensor(name, shape, dt))

        def sem(name):
            return ctx.enter_context(nc.semaphore(name))

        XS = PIX
        Xm = sb("Xm", [128, NX * XS])
        Xt = sb("Xt", [128, NX * XS // 2])
        x1m = sb("x1m", [128, 2 * MAIN_ROWS * XW])
        x1t = sb("x1t", [128, 2 * TAIL_ROWS * XW])
        XN = WIN * WP
        nm = sb("nm", [128, TOK])
        nt = sb("nt", [TAIL, TOK])
        xmh = sb("xmh", [128, XN], f32r)
        xml = sb("xml", [128, XN], f32r)
        xts = sb("xts", [128, XN], f32r)
        qm = sb("qm", [128, 2, TOK])
        km = sb("km", [128, 2, TOK])
        qt = sb("qt", [TAIL, 2, TOK])
        kt = sb("kt", [TAIL, 2, TOK])
        V = sb("V", [128, 2, WIN, 3, 64])
        sT = sb("sT", [128, 2, 2, HEADS * L])
        mx = sb("mx", [128, 2, 2 * HEADS])
        sm = sb("sm", [128, 2, 2 * HEADS])
        rc = sb("rc", [128, 2, 2 * HEADS])
        P = sb("P", [128, 2, 4 * HEADS * 64])
        PT = sb("PT", [128, 2, 3 * 2 * L])
        omh = sb("omh", [128, TOK], f32r)
        oml = sb("oml", [128, TOK], f32r)
        ots = sb("ots", [128, TOK], f32r)
        ym = sb("ym", [128, 2, 8 * WW])
        yt = sb("yt", [128, 2, TAIL_STEP * WW])
        prod = sb("prod", [128, 7, TAIL_STEP * WW])
        b0 = prod[:, 0:2, :].rearrange("p a b -> p (a b)")[:, 0:HEADS * L].rearrange("p (h j) -> p h j", j=L)
        mk = prod[:, 2, 0:4 * L].rearrange("p (a b j) -> p a b j", a=2, b=2)
        NW = 3 * CH
        NWP = NW + CH + TAIL
        wf = P[:, :, :].rearrange("p a b -> p (a b)")[:, 0:2 * NWP].rearrange("p (t c) -> p t c", t=2)
        wmh = sb("wmh", [128, NW + CH + TAIL], f32r)
        wml = sb("wml", [128, NW + CH + TAIL], f32r)
        wth = sb("wth", [128, NW + CH + TAIL], f32r)
        wtl = sb("wtl", [128, NW + CH + TAIL], f32r)
        vec = sb("vec", [128, 12])
        zeros = sb("zeros", [128, 2 * MAIN_ROWS])
        BM = sb("BM", [128, 2, 2, HEADS * L])
        G = sb("G", [128, 2, 256])
        cw = sb("cw", [128, 2, 9])
        tick = sb("tick", [128, 3])
        ident = sb("ident", [128, 128])
        half = sb("half", [128, 2])
        bp = sb("bp", [128, 2])
        bq = sb("bq", [128, 2])
        bpc = sb("bpc", [128, 2])
        wsum = sb("wsum", [128, 2])
        st1 = sb("st1", [128, 2, STRIPS, 6])
        st2 = sb("st2", [128, 2, STRIPS + 1, 6])
        mv = sb("mv", [128, 2, 2, 2])
        dv = sb("dv", [128, 2, 2])
        t2 = sb("t2", [128, 2, 2])
        gme = sb("gme", [128, 2, 2])
        gve = sb("gve", [128, 2, 2])
        rs = sb("rs", [128, 2, 2])
        nb1 = sb("nb1", [128, 2])
        mfill = sb("mfill", [128, 2])
        ms = sb("ms", [128, 2])
        mw = sb("mw", [128, 2])
        weff = sb("weff", [128, 2, 9])
        b2 = sb("b2", [128, 2])

        def bank(name, n=1):
            return ctx.enter_context(nc.psum_tensor(name, [128, n, 512], f32))

        psS, psT, psO, psR = bank("psS", 4), bank("psT"), bank("psO", 2), bank("psR")
        ST0 = 400

        x_loaded = sem("x_loaded")
        consts = sem("consts")
        ticked = sem("ticked")
        setup_dve = sem("setup_dve")
        setup_pe = sem("setup_pe")
        wsplit = sem("wsplit")
        x_stats = sem("x_stats")
        normed = sem("normed")
        high = sem("high")
        low_m = sem("low_m")
        low_t = sem("low_t")
        qk_done = sem("qk_done")
        v_done = sem("v_done")
        qk_out = sem("qk_out")
        v_out = sem("v_out")
        s_done = sem("s_done")
        biased = sem("biased")
        maxed = sem("maxed")
        centred = sem("centred")
        exped = sem("exped")
        summed = sem("summed")
        recip = sem("recip")
        probs = sem("probs")
        pt_done = sem("pt_done")
        pt_out = sem("pt_out")
        av_done = sem("av_done")
        o_high = sem("o_high")
        o_low = sem("o_low")
        proj_done = sem("proj_done")
        resid = sem("resid")
        x1_stats = sem("x1_stats")
        gn = [sem("gn1"), sem("gn2")]
        gn_pe = [sem("gn1_pe"), sem("gn2_pe")]
        gn_pow = [sem("gn1_pow"), sem("gn2_pow")]
        fixed = sem("fixed")
        conv_m = sem("conv_m")
        prods = sem("prods")
        conv_p = sem("conv_p")
        stored = [sem("stored0"), sem("stored1")]
        stored_t = [sem("stored_t0"), sem("stored_t1")]
        GN_DVE = [9, 15]
        FIX = 12

        def upto(per, strip, part, last=ALL - 1):
            if isinstance(strip, int):
                if strip < 0:
                    return 0
                if strip > last:
                    strip, part = last, per
            return strip * per + part

        def settle(eng):
            eng.reg_alu(scratch[eng], scratch[eng], 0, ALU.add)

        scratch = {}

        def tok(v):
            return v.rearrange("p (w t) -> p w t", t=WP)[:, :, 0:L]

        def wt(v):
            return v.rearrange("p (w t) -> p w t", t=L)

        def xmain(n, r):
            return Xm[:, bass.ds((n % NX) * XS + r * TOK, TOK)]

        def xtail(n, r, p0=None, p1=None):
            p = 0 if r < STRIPS // 2 else 64
            p0, p1 = (p, p + 64) if p0 is None else (p0, p1)
            return Xt[p0:p1, bass.ds((n % NX) * (XS // 2) + r % (STRIPS // 2) * TOK, TOK)]

        def grid(buf, p0, p1, base, rows, r0, nr, c0, ncol):
            v = buf[p0:p1, bass.ds(base, rows * XW)]
            return v.rearrange("p (r c) -> p r c", c=XW)[:, r0:r0 + nr, c0:c0 + ncol]

        def x1main(n, r0, nr, c0, ncol):
            return grid(x1m, 0, 128, (n % 2) * (MAIN_ROWS * XW), MAIN_ROWS, r0, nr, c0, ncol)

        def x1tail(n, p0, p1, r0, nr, c0, ncol):
            return grid(x1t, p0, p1, (n % 2) * (TAIL_ROWS * XW), TAIL_ROWS, r0, nr, c0, ncol)

        def stage(t_img, r, lag):
            k = r - lag
            return t_img + k // STRIPS, k % STRIPS

        def live(n, r):
            return not isinstance(n, int) or (0 <= n < IMAGES)

        def product(r, i):
            if r == STRIPS - 1:
                return prod[:, i // TAIL_STEP, i % TAIL_STEP * WW:(i % TAIL_STEP + 1) * WW]
            return prod[:, HOLD[i], :]

        def closes(n, r):
            return r == STRIPS - 1 and live(n, r)

        def gidx(n, r):
            return n * STRIPS + r

        def schedule(eng, slot):
            scratch[eng] = eng.alloc_register("settle")
            eng.reg_mov(scratch[eng], 0)
            for n in (-2, -1, 0, 1):
                for r in range(STRIPS):
                    slot(n, r)
            with eng.Fori(2, IMAGES - 2, 1) as n:
                for r in range(STRIPS):
                    slot(n, r)
            for n in range(IMAGES - 2, IMAGES + 2):
                for r in range(STRIPS):
                    slot(n, r)

        vq, vk, vv, vpj, vcv = (vec[:, i:i + 2] for i in (0, 2, 4, 6, 8))
        SETUP = 5
        block = ctx.enter_context(nc.Block())

        @block.sync
        def _(sp):
            for dst, src in ((wf[:, 0, :], wqkv[0:128, :]), (wf[0:64, 1, :], wqkv[128:192, :]),
                             (wf[64:128, 1, :], wqkv[128:192, :]), (vec[:, :], vecs),
                             (b0[:, :, :], bias), (mk[:, :, :, :], mask), (G[:, :, :], gavg), (cw[:, :, :], convw),
                             (ident[:, :], ident_d)):
                sp.dma_start(dst, src).then_inc(consts, 16)

            def slot(n, r):
                m = n + 2
                if r == 3 and live(m, 0):
                    sp.wait_ge(x_loaded, upto(48, m - 1, 48, IMAGES - 1))
                    sp.wait_ge(resid, upto(4, gidx(m - NX, STRIPS - 1), 4))
                    load(m)
                cn, cr = stage(n, r, LAG_CONV)
                if live(cn, cr):
                    g = gidx(cn, cr)
                    b = cr % 2
                    rows = WS + (cr == STRIPS - 1)
                    sp.wait_ge(conv_m, upto(9, g, 9))
                    sp.dma_start(y_main[cn, :, cr * TOK:cr * TOK + rows * WW],
                                 ym[:, b, 0:rows * WW]).then_inc(stored[b], 16)
                cn, cr = stage(n, r, LAG_TAIL)
                if live(cn, cr):
                    g = gidx(cn, cr)
                    b = cr % 2
                    tr = TAIL_STEP if cr < STRIPS - 1 else 1
                    sp.wait_ge(conv_p, upto(8, g, 8))
                    sp.dma_start(y_tail[cn, :, cr * TAIL_STEP * WW:(cr * TAIL_STEP + tr) * WW],
                                 yt[:, b, 0:tr * WW]).then_inc(stored_t[b], 16)

            def load(m):
                sp.dma_start(Xm[:, bass.ds((m % NX) * XS, PIX)], x[m, 0:128, :]).then_inc(x_loaded, 16)
                half = PIX // 2
                for p0, c0 in ((0, 0), (64, half)):
                    sp.dma_start(Xt[p0:p0 + 64, bass.ds((m % NX) * half, half)],
                                 x[m, 128:192, c0:c0 + half]).then_inc(x_loaded, 16)

            schedule(sp, slot)
            for b in range(2):
                sp.wait_ge(stored[b], 16 * (ALL // 2))
                sp.wait_ge(stored_t[b], 16 * (ALL // 2))

        @block.tensor
        def _(pe):
            mm = nc.tensor.matmul

            def split5(out, wc, rhs_m, rhs_ml, rhs_t, w_first):
                terms = ((wmh[:, wc], rhs_m), (wml[:, wc], rhs_m), (wmh[:, wc], rhs_ml),
                         (wth[:, wc], rhs_t), (wtl[0:64, wc], rhs_t[0:64]))
                for i, (w, v) in enumerate(terms):
                    a, b = (w, v) if w_first else (v, w)
                    last = mm(out, a, b, start=(i == 0), stop=(i == 4))
                return last

            pe.wait_ge(consts, 16 * 9)
            pe.wait_ge(setup_dve, 1)
            for tl, c0 in ((0, NW), (1, NW + 128)):
                mm(psT[:, 0, ST0 + tl:ST0 + tl + 1], wf[:, 0, c0:c0 + 128], vv[:, 0:1], start=True, stop=False)
                last = mm(psT[:, 0, ST0 + tl:ST0 + tl + 1], wf[0:64, 1, c0:c0 + 128], vv[0:64, 1:2], start=False, stop=True)
            last.then_inc(setup_pe, 1)
            pe.wait_ge(wsplit, 4)

            def scores(n, r, h):
                g = gidx(n, r)
                if h == 0:
                    pe.wait_ge(qk_out, upto(4, g, 4))
                    pe.wait_ge(biased, upto(4, g - 1, 4))
                else:
                    pe.wait_ge(biased, upto(4, g, 2))
                for pair in (2 * h, 2 * h + 1):
                    for w in range(2):
                        c0 = (pair * 2 + w) * L
                        for hd in range(HEADS):
                            q, k, p = (qm, km, 32 * hd) if hd < 4 else (qt, kt, 32 * (hd - 4))
                            col = (hd // 4 * 4 + pair) * L
                            last = mm(psS[64 * w:64 * w + L, hd % 4, col:col + L],
                                      q[p:p + 32, r % 2, c0:c0 + L],
                                      k[p:p + 32, r % 2, c0:c0 + L],
                                      start=True, stop=True)
                last.then_inc(s_done, 1)

            def transpose_probs(n, r, pair):
                g = gidx(n, r)
                pe.wait_ge(probs, upto(2, g, pair // 2 + 1))
                pe.wait_ge(pt_out, upto(4, g, pair)) if pair else pe.wait_ge(pt_out, upto(4, g - 1, 4))
                for q in range(3):
                    c0 = (pair * HEADS + 2 * q) * 64
                    last = nc.tensor.transpose(psT[:, 0, q * 128:q * 128 + 128],
                                               P[:, r % 2, c0:c0 + 128], ident[:, :])
                last.then_inc(pt_done, 1)

            def attend(n, r, pair):
                g = gidx(n, r)
                pe.wait_ge(pt_out, upto(4, g, pair + 1))
                if pair == 0:
                    pe.wait_ge(v_out, upto(8, g, 8))
                    pe.wait_ge(resid, upto(4, g - 1, 4))
                for w in range(2):
                    wi = pair * 2 + w
                    for q in range(3):
                        out = psO[64 * (q % 2):64 * (q % 2) + 64, q // 2, wi * L:wi * L + L]
                        p0 = (q * 2 + w) * L
                        last = mm(out, V[:, r % 2, wi, q, :], PT[:, pair % 2, p0:p0 + L],
                                  start=True, stop=True)
                last.then_inc(av_done, 1)

            def qk(n, r, j):
                g = gidx(n, r)
                if j == 0:
                    pe.wait_ge(high, upto(2, g, 2))
                    pe.wait_ge(low_m, upto(1, g, 1))
                    pe.wait_ge(low_t, upto(1, g, 1))
                    pe.wait_ge(v_out, upto(8, g - 1, 8))
                else:
                    pe.wait_ge(qk_out, upto(4, g, j))
                split5(psR[:, 0, 0:WIN * WN], slice(128 * j, 128 * j + 128), even(xmh),
                       even(xml), even(xts), True).then_inc(qk_done, 1)

            def even(buf):
                return buf[:, :].rearrange("k (w t) -> k w t", t=WP)[:, :, 0:WN]

            def windows(buf, p):
                return buf[:, p * 2 * WP:(p + 1) * 2 * WP]

            def values(n, r, i):
                g = gidx(n, r)
                if i:
                    pe.wait_ge(v_out, upto(8, g, 4))
                else:
                    pe.wait_ge(qk_out, upto(4, g, 4))
                for pr in range(2):
                    p = 2 * i + pr
                    last = split5(psR[:, 0, pr * CH:pr * CH + CH], slice(2 * CH, 3 * CH),
                                  windows(xmh, p), windows(xml, p), windows(xts, p), False)
                last.then_inc(v_done, 1)

            def project(n, r):
                g = gidx(n, r)
                pe.wait_ge(o_high, upto(2, g, 2))
                pe.wait_ge(o_low, upto(2, g, 2))
                for tl in range(2):
                    c0 = NW + 128 * tl
                    split5(psO[:, tl, 0:TOK], slice(c0, c0 + 128), omh[:, :], oml[:, :], ots[:, :],
                           True).then_inc(proj_done, 1)

            def averages(k, n, i):
                src = t2[:, k, :] if i else mv[:, k, :, 0]
                pe.wait_ge(gn[k], upto(GN_DVE[k], n, (3 + k, 7 + k)[i], IMAGES - 1))
                for tl in range(2):
                    c0 = ST0 + 8 * k + 4 * i + tl
                    o = psS[:, 0, c0:c0 + 1]
                    mm(o, G[:, 0, 128 * tl:128 * tl + 128], src[:, 0:1], start=True, stop=False)
                    last = mm(o, G[:, 1, 128 * tl:128 * tl + 128], src[:, 1:2], start=False, stop=True)
                last.then_inc(gn_pe[k], 1)

            def slot(n, r):
                s, o, b, p = stage(n, r, LAG_SCORES), stage(n, r, LAG_OUT), (n, r), stage(n, r, LAG_PROJ)
                a1, a2 = stage(n, r, LAG_STATS + 1), stage(n, r, LAG_STATS + 2)
                p1 = stage(n, r, LAG_PROJ + 1)
                if closes(*p1):
                    averages(1, p1[0], 1)
                if closes(*a1):
                    averages(0, a1[0], 0)
                if closes(*a2):
                    pe.wait_ge(gn[0], upto(GN_DVE[0], a2[0], 8, IMAGES - 1))
                if live(*s):
                    scores(*s, 0)
                if live(*p):
                    project(*p)
                for pair in range(4):
                    if live(*b):
                        if pair < 3:
                            qk(*b, pair)
                        else:
                            values(*b, 0)
                    if live(*o):
                        attend(*o, pair)
                        if pair < 3:
                            transpose_probs(*o, pair + 1)
                    if pair == 1:
                        if closes(*p1):
                            pe.wait_ge(gn[1], upto(GN_DVE[1], p1[0], 9, IMAGES - 1))
                        if closes(*a1):
                            averages(0, a1[0], 1)
                        if closes(*p):
                            averages(1, p[0], 0)
                        if live(*s):
                            scores(*s, 1)
                if live(*s):
                    transpose_probs(*s, 0)
                if live(*b):
                    values(*b, 1)

            schedule(pe, slot)

        @block.scalar
        def _(act):
            A = nc.scalar.activation
            act.wait_ge(setup_dve, SETUP)

            def normalise(n, r):
                g = gidx(n, r)
                act.wait_ge(gn[0], upto(GN_DVE[0], n, GN_DVE[0], IMAGES - 1))
                act.wait_ge(low_m, upto(1, g - 1, 1))
                act.wait_ge(low_t, upto(1, g - 1, 1))
                act.wait_ge(x_loaded, upto(48, n, 48, IMAGES - 1))
                if not isinstance(n, int):
                    settle(act)
                A(wt(nm[:, :]), wt(xmain(n, r)), ACT.Identity, scale=rs[:, 0, 0:1],
                  bias=nb1[:, 0:1]).then_inc(normed, 1)
                p0 = 0 if r < STRIPS // 2 else 64
                A(wt(nt[:, :]), wt(xtail(n, r)), ACT.Identity, scale=rs[p0:p0 + 64, 0, 1:2],
                  bias=nb1[p0:p0 + 64, 1:2]).then_inc(normed, 1)

            def split(n, r):
                g = gidx(n, r)
                act.wait_ge(normed, upto(2, g, 1))
                act.wait_ge(v_done, upto(2, g - 1, 2))
                A(tok(xmh[:, :]), wt(nm[:, :]), ACT.Copy).then_inc(high, 1)
                act.wait_ge(normed, upto(2, g, 2))
                A(tok(xts[0:64, :]), wt(nt[:, :]), ACT.Copy).then_inc(high, 1)

            def win50(v):
                return v.rearrange("p (w t) -> p w t", t=WN)[:, :, 0:L]

            def evacuate_qk(n, r, j):
                g = gidx(n, r)
                act.wait_ge(qk_done, upto(3, g, j + 1))
                if j == 0:
                    act.wait_ge(s_done, upto(2, g - 2, 2))
                if j == 0:
                    A(wt(qm[:, r % 2, :]), win50(psR[:, 0, 0:WIN * WN]), ACT.Identity, scale=SCALE,
                      bias=bq[:, 0:1]).then_inc(qk_out, 1)
                elif j == 1:
                    A(wt(km[:, r % 2, :]), win50(psR[:, 0, 0:WIN * WN]), ACT.Identity, bias=vk[:, 0:1]).then_inc(qk_out, 1)
                else:
                    A(wt(qt[:, r % 2, :]), win50(psR[0:64, 0, 0:WIN * WN]), ACT.Identity, scale=SCALE,
                      bias=bq[0:64, 1:2]).then_inc(qk_out, 1)
                    A(wt(kt[:, r % 2, :]), win50(psR[64:128, 0, 0:WIN * WN]), ACT.Identity,
                      bias=vec[64:128, 3:4]).then_inc(qk_out, 1)

            def evacuate_v(n, r, i):
                g = gidx(n, r)
                act.wait_ge(v_done, upto(2, g, i + 1))
                act.wait_ge(av_done, upto(4, g - 2, 2 * i + 2))
                for w in range(2):
                    for odd in range(2):
                        src = psR[64 * w:64 * w + 64, 0, 0:2 * CH].rearrange(
                            "p (a q e d) -> p a q e d", a=2, q=3, e=2)[:, :, :, odd, :]
                        dst = V[64 * odd:64 * odd + 64, r % 2, 4 * i + w:4 * i + w + 3:2, :,
                                32 * odd:32 * odd + 32]
                        A(dst, src, ACT.Copy).then_inc(v_out, 1)

            def exponentials(n, r, h):
                g = gidx(n, r)
                act.wait_ge(centred, upto(2, g, h + 1))
                act.wait_ge(pt_done, upto(4, g - 2, 2 * h + 2))
                dst = P[:, r % 2, h * 2 * HEADS * 64:(h + 1) * 2 * HEADS * 64].rearrange(
                    "p (s j) -> p s j", j=64)[:, :, 0:L]
                A(dst, sT[:, h, :, :].rearrange("p a (s j) -> p (a s) j", j=L),
                  ACT.Exp).then_inc(exped, 1)

            def evacuate_pt(n, r, pair):
                g = gidx(n, r)
                act.wait_ge(pt_done, upto(4, g, pair + 1))
                act.wait_ge(av_done, upto(4, g, pair - 1)) if pair > 1 else act.wait_ge(av_done, upto(4, g - 1, pair + 3))
                src = psT[:, 0, 0:384].rearrange("p (s i) -> p s i", i=64)[:, :, 0:L]
                A(PT[:, pair % 2, :].rearrange("p (s i) -> p s i", i=L), src,
                  ACT.Copy).then_inc(pt_out, 1)

            def evacuate_o(n, r):
                g = gidx(n, r)
                act.wait_ge(av_done, upto(4, g, 4))
                act.wait_ge(proj_done, upto(2, g - 1, 2))
                A(omh[:, :], psO[:, 0, 0:TOK], ACT.Copy).then_inc(o_high, 1)
                A(ots[0:64, :], psO[0:64, 1, 0:TOK], ACT.Copy).then_inc(o_high, 1)

            def products(n, r, k):
                g = gidx(n, r)
                rows = TAIL_STEP if r < STRIPS - 1 else 1

                def shifted(tap):
                    return x1tail(n, 0, 128, TAIL_STEP * r + tap // 3, rows, tap % 3, WW)

                if k == 0:
                    act.wait_ge(fixed, upto(FIX, n, FIX, IMAGES - 1))
                    act.wait_ge(conv_p, upto(8, g - 1, GROUPS[0][1] if r else 8))
                    if not isinstance(n, int) or g >= 2:
                        act.wait_ge(stored_t[r % 2], g * 8 - 8 * (r % 2))
                elif r < STRIPS - 1 and k == 1:
                    act.wait_ge(conv_p, upto(8, g - 1, 8))
                elif r < STRIPS - 1:
                    act.wait_ge(conv_p, upto(8, g, HOLD[7] + 1))
                if not isinstance(n, int) and (k == 0 or r < STRIPS - 1):
                    settle(act)
                if k == 0:
                    A(yt[:, r % 2, 0:rows * WW].rearrange("p (a b) -> p a b", b=WW), shifted(TAPS[0]),
                      ACT.Identity, scale=weff[:, 1, TAPS[0]:TAPS[0] + 1], bias=b2[:, 1:2]).then_inc(prods, 1)
                for i in range(*GROUPS[k]):
                    tap = TAPS[1 + i]
                    A(product(r, i).rearrange("p (a b) -> p a b", b=WW), shifted(tap),
                      ACT.Copy, scale=weff[:, 1, tap:tap + 1]).then_inc(prods, 1)

            def slot(n, r):
                s, o, b, c = stage(n, r, LAG_SCORES), stage(n, r, LAG_OUT), (n, r), stage(n, r, LAG_TAIL)
                m = stage(n, r, LAG_NORM)
                if live(*c):
                    for k in range(3 if closes(*c) else 1):
                        products(*c, k)
                if live(*b):
                    evacuate_qk(*b, 0)
                if live(*o):
                    evacuate_pt(*o, 1)
                if live(*m):
                    normalise(*m)
                if live(*b):
                    evacuate_qk(*b, 1)
                if live(*s):
                    exponentials(*s, 0)
                if live(*o):
                    evacuate_pt(*o, 2)
                if live(*c) and not closes(*c):
                    products(*c, 1)
                if live(*b):
                    evacuate_qk(*b, 2)
                if live(*o):
                    evacuate_pt(*o, 3)
                if live(*b):
                    evacuate_v(*b, 0)
                if live(*o):
                    evacuate_o(*o)
                if live(*s):
                    exponentials(*s, 1)
                    evacuate_pt(*s, 0)
                if live(*b):
                    evacuate_v(*b, 1)
                if live(*m):
                    split(*m)
                if live(*c) and not closes(*c):
                    products(*c, 2)

            schedule(act, slot)

        @block.gpsimd
        def _(pool):
            TT = nc.gpsimd.tensor_tensor
            nc.gpsimd.memset(half[:, :], -0.5).then_inc(wsplit, 1)
            pool.wait_ge(setup_dve, SETUP)
            pool.wait_ge(wsplit, 4)

            def per_head(v):
                return v.unsqueeze(2).to_broadcast([128, 2 * HEADS, L])

            def centre(n, r, h):
                g = gidx(n, r)
                pool.wait_ge(maxed, upto(2, g, h + 1))
                v = sT[:, h, :, :].rearrange("p a (s j) -> p (a s) j", j=L)
                TT(v, v, per_head(mx[:, h, :]), ALU.subtract).then_inc(centred, 1)

            def normalise(n, r, h):
                g = gidx(n, r)
                pool.wait_ge(recip, upto(2, g, h + 1))
                v = P[:, r % 2, h * 2 * HEADS * 64:(h + 1) * 2 * HEADS * 64].rearrange(
                    "p (s j) -> p s j", j=64)[:, :, 0:L]
                TT(v, v, per_head(rc[:, h, :]), ALU.mult).then_inc(probs, 1)

            def low(n, r):
                g = gidx(n, r)
                pool.wait_ge(high, upto(2, g, 1))
                pool.wait_ge(v_done, upto(2, g - 1, 2))
                TT(tok(xml[:, :]), wt(nm[:, :]), tok(xmh[:, :].bitcast(f32)), ALU.subtract).then_inc(low_m, 1)

            def add_products(n, r, k):
                g = gidx(n, r)
                rows = TAIL_STEP if r < STRIPS - 1 else 1
                acc = yt[:, r % 2, 0:rows * WW]
                for i in range(*GROUPS[k]):
                    pool.wait_ge(prods, upto(9, g, i + 2))
                    if i:
                        pool.wait_ge(conv_p, upto(8, g, i))
                    TT(acc, acc, product(r, i), ALU.add).then_inc(conv_p, 1)

            def power(k, n):
                pool.wait_ge(gn[k], upto(GN_DVE[k], n, 8 + k, IMAGES - 1))
                if k == 0:
                    pool.wait_ge(normed, upto(2, gidx(n - 1, STRIPS - 1), 2))
                TT(rs[:, k, :], gve[:, k, :], half[:, :], ALU.pow).then_inc(gn_pow[k], 1)

            def slot(n, r):
                s, m, c = stage(n, r, LAG_SCORES), stage(n, r, LAG_NORM), stage(n, r, LAG_TAIL)
                a1, p1 = stage(n, r, LAG_STATS + 1), stage(n, r, LAG_PROJ + 1)
                if closes(*p1):
                    power(1, p1[0])
                if live(*s):
                    centre(*s, 0)
                if live(*c):
                    for k in range(3 if closes(*c) else 1):
                        add_products(*c, k)
                if live(*s):
                    normalise(*s, 0)
                    centre(*s, 1)
                if closes(*a1):
                    power(0, a1[0])
                if live(*c) and not closes(*c):
                    add_products(*c, 1)
                if live(*m):
                    low(*m)
                if live(*s):
                    normalise(*s, 1)
                if live(*c) and not closes(*c):
                    add_products(*c, 2)

            schedule(pool, slot)

        @block.vector
        def _(dve):
            v_ = nc.vector
            for ps in (psS, psT, psO, psR):
                last = v_.memset(ps[:, :, :], 0.0)
            last.then_inc(setup_dve, 1)
            for buf in (x1m, x1t):
                v_.memset(buf[:, :], 0.0)
            v_.memset(V[:, :, :, :, :], 0.0)
            for buf in (st1, st2):
                v_.memset(buf[:, :, :, :], 0.0)
            for buf in (mv,):
                v_.memset(buf[:, :, :, :], 0.0)
            v_.memset(zeros[:, :], 0.0)
            for buf in (xmh, xml, xts):
                v_.memset(buf[:, :].bitcast(f32), 0.0)
            v_.memset(t2[:, :, :], 0.0).then_inc(setup_dve, 1)
            dve.wait_ge(setup_dve, 2)
            dve.wait_ge(consts, 16 * 9)
            for row in range(2):
                for col in range(2):
                    v_.tensor_tensor(BM[:, row, col, :].rearrange("p (h j) -> p h j", j=L), b0[:, :, :],
                                     mk[:, row, col, :].unsqueeze(1).to_broadcast([128, HEADS, L]), ALU.add)
            v_.tensor_copy(wmh[:, :], wf[:, 0, :])
            v_.tensor_copy(wth[:, :], wf[:, 1, :]).then_inc(setup_dve, 1)
            dve.wait_ge(setup_dve, 3)
            v_.tensor_tensor(wml[:, :], wf[:, 0, :], wmh[:, :].bitcast(f32), ALU.subtract).then_inc(wsplit, 1)
            v_.tensor_tensor(wtl[:, :], wf[:, 1, :], wth[:, :].bitcast(f32), ALU.subtract).then_inc(wsplit, 1)
            v_.tensor_scalar(bq[:, :], vq, SCALE, None, ALU.mult).then_inc(wsplit, 1)
            dve.wait_ge(setup_pe, 1)
            v_.tensor_tensor(bp[:, :], psT[:, 0, ST0:ST0 + 2], vpj, ALU.add)
            dve.wait_ge(wsplit, 4)
            v_.memset(P[:, :, :], 0.0)
            v_.reduce_sum(wsum[:, :], cw[:, :, :], AX.X).then_inc(setup_dve, 1)
            dve.wait_ge(setup_dve, 4)
            v_.tensor_tensor(bpc[:, :], bp[:, :], vcv, ALU.add).then_inc(setup_dve, 1)
            dve.wait_ge(setup_dve, 5)

            def x_statistics(n, r):
                g = gidx(n, r)
                if r == 0:
                    dve.wait_ge(ticked, upto(1, n - 1, 1, IMAGES - 1))
                    dve.wait_ge(x_loaded, upto(48, n, 48, IMAGES - 1))
                    dve.wait_ge(gn[0], upto(GN_DVE[0], n - 1, 3, IMAGES - 1))
                    v_.tensor_copy(tick[:, 2:3], zeros[:, 0:1]).then_inc(ticked, 1)
                if r < STRIPS // 2:
                    v_.bn_stats(st1[:, 1, r, :], xtail(n, r, 0, 128)).then_inc(x_stats, 1)
                v_.bn_stats(st1[:, 0, r, :], xmain(n, r)).then_inc(x_stats, 1 if r < STRIPS // 2 else 2)

            def low_tail(n, r):
                g = gidx(n, r)
                dve.wait_ge(high, upto(2, g, 2))
                dve.wait_ge(v_done, upto(2, g - 1, 2))
                v_.tensor_tensor(tok(xts[64:128, :]), wt(nt[:, :]), tok(xts[0:64, :].bitcast(f32)),
                                 ALU.subtract).then_inc(low_t, 1)

            def add_bias(n, r, h):
                g = gidx(n, r)
                dve.wait_ge(s_done, upto(2, g, h + 1))
                dve.wait_ge(exped, upto(2, g - 1, h + 1))
                row = int(r == STRIPS - 1)
                table = BM[:, row, 0:1, :].to_broadcast([128, 2, HEADS * L]) if h == 0 else BM[:, row, :, :]
                for h0, h1, c0 in ((0, 4, 2 * h * L), (4, 6, (4 + 2 * h) * L)):
                    out, tab = (v[:, :, h0 * L:h1 * L].rearrange("p a (s j) -> p a s j", j=L)
                                for v in (sT[:, h, :, :], table))
                    src = psS[:, 0:h1 - h0, c0:c0 + 2 * L].rearrange("p s (a j) -> p a s j", a=2)
                    v_.tensor_tensor(out, src, tab, ALU.add).then_inc(biased, 1)

            def maxima(n, r, h):
                g = gidx(n, r)
                dve.wait_ge(biased, upto(4, g, 2 * h + 2))
                dve.wait_ge(centred, upto(2, g - 1, h + 1))
                v_.reduce_max(mx[:, h, :], sT[:, h, :, :].rearrange("p a (s j) -> p (a s) j", j=L),
                              AX.X).then_inc(maxed, 1)

            def sums(n, r, h):
                g = gidx(n, r)
                dve.wait_ge(exped, upto(2, g, h + 1))
                src = P[:, r % 2, h * 2 * HEADS * 64:(h + 1) * 2 * HEADS * 64].rearrange(
                    "p (s j) -> p s j", j=64)[:, :, 0:L]
                v_.reduce_sum(sm[:, h, :], src, AX.X).then_inc(summed, 1)

            def reciprocals(n, r, h):
                g = gidx(n, r)
                dve.wait_ge(summed, upto(2, g, h + 1))
                dve.wait_ge(probs, upto(2, g - 1, h + 1))
                v_.reciprocal(rc[:, h, :], sm[:, h, :]).then_inc(recip, 1)

            def o_lows(n, r):
                g = gidx(n, r)
                dve.wait_ge(o_high, upto(2, g, 1))
                dve.wait_ge(proj_done, upto(2, g - 1, 2))
                v_.tensor_tensor(oml[:, :], psO[:, 0, 0:TOK], omh[:, :].bitcast(f32), ALU.subtract).then_inc(o_low, 1)
                dve.wait_ge(o_high, upto(2, g, 2))
                v_.tensor_tensor(ots[64:128, :], psO[0:64, 1, 0:TOK], ots[0:64, :].bitcast(f32),
                                 ALU.subtract).then_inc(o_low, 1)

            def residual(n, r):
                g = gidx(n, r)
                dve.wait_ge(proj_done, upto(2, g, 1))
                if r == 0:
                    dve.wait_ge(conv_m, upto(9, gidx(n - 2, STRIPS - 1), 9))
                    dve.wait_ge(prods, upto(9, gidx(n - 2, STRIPS - 1), 9))
                r0 = WS * r
                cut = 53 - r0 if r == STRIPS - 1 else WS

                def win(v, a0, a1):
                    return v.rearrange("p (w a b) -> p w a b", a=WS, b=WS)[:, :, a0:a1, :]

                def rows(v):
                    return v.rearrange("p a (w b) -> p w a b", b=WS)

                def part(tile_, a0, a1):
                    if tile_ == 0:
                        dst = x1main(n, 1 + r0 + a0 + (a0 >= cut), a1 - a0, 4, WW)
                        src, xin = psO[:, 0, 0:TOK], xmain(n, r)
                    else:
                        up = r < STRIPS // 2
                        row = 1 + r0 + a0 + (a0 >= cut) - (0 if up else HALF)
                        dst = x1tail(n, 0 if up else 64, 64 if up else 128, row, a1 - a0, 4, WW)
                        src, xin = psO[0:64, 1, 0:TOK], xtail(n, r)
                    return v_.tensor_tensor(rows(dst), win(src, a0, a1), win(xin, a0, a1), ALU.add)

                for tl in range(2):
                    if tl:
                        dve.wait_ge(proj_done, upto(2, g, 2))
                    if cut < WS:
                        part(tl, 0, cut).then_inc(resid, 1)
                        part(tl, cut, WS).then_inc(resid, 1)
                    else:
                        part(tl, 0, WS).then_inc(resid, 2)

            def x1_statistics(n, r):
                r0 = WS * r
                pad = r == STRIPS - 1
                p0 = 0 if r < STRIPS // 2 else 64
                row = 1 + r0 - (HALF if p0 else 0)
                rr = r % (STRIPS // 2)
                for a0, a1, more in [(0, 4, 0), (4, WS, 1)] if pad else [(0, WS, 0)]:
                    i1 = v_.bn_stats(st2[:, 0, r + more, :], x1main(n, 1 + r0 + a0 + more, a1 - a0, 4, WW))
                for a0, a1, more in [(0, 4, 0), (4, WS, 1)] if rr == 3 else [(0, WS, 0)]:
                    i2 = v_.bn_stats(st2[p0:p0 + 64, 1, rr + more, :],
                                     x1tail(n, p0, p0 + 64, row + a0 + (more if pad else 0), a1 - a0, 4, WW))
                i1.then_inc(x1_stats, 1)
                i2.then_inc(x1_stats, 1)

            def norm_gather(k, n):
                dve.wait_ge(gn[k], upto(GN_DVE[k], n - 1, GN_DVE[k], IMAGES - 1))
                dve.wait_ge((x_stats, x1_stats)[k], upto(2, gidx(n, STRIPS - 1), 2))
                v_.tensor_copy(tick[:, k:k + 1], zeros[:, 0:1]).then_inc(gn[k], 1)
                if k == 0:
                    v_.bn_aggr(mv[:, 0, 0, :], st1[:, 0, :, :]).then_inc(gn[k], 1)
                    v_.bn_aggr(mv[:, 0, 1, :], st1[:, 1, 0:STRIPS // 2, :]).then_inc(gn[k], 1)
                else:
                    v_.bn_aggr(mv[:, 1, 0, :], st2[:, 0, 0:9, :]).then_inc(gn[k], 1)
                    v_.bn_aggr(mv[:, 1, 1, :], st2[:, 1, 0:5, :]).then_inc(gn[k], 1)
                    dve.wait_ge(gn[k], upto(GN_DVE[k], n, 3, IMAGES - 1))
                    v_.tensor_tensor(mv[:, 1, :, 0], mv[:, 1, :, 0], bp[:, :], ALU.add).then_inc(gn[k], 1)

            def norm_mean(k, n):
                c0 = ST0 + 8 * k
                dve.wait_ge(gn_pe[k], upto(2, n, 1, IMAGES - 1))
                v_.tensor_copy(gme[:, k, :], psS[:, 0, c0:c0 + 2]).then_inc(gn[k], 1)
                v_.tensor_tensor(dv[:, k, :], mv[:, k, :, 0], psS[:, 0, c0:c0 + 2], ALU.subtract).then_inc(gn[k], 1)
                dve.wait_ge(gn[k], upto(GN_DVE[k], n, 5 + k, IMAGES - 1))
                v_.tensor_tensor(t2[:, k, :], dv[:, k, :], dv[:, k, :], ALU.mult).then_inc(gn[k], 1)
                dve.wait_ge(gn[k], upto(GN_DVE[k], n, 6 + k, IMAGES - 1))
                v_.tensor_tensor(t2[:, k, :], t2[:, k, :], mv[:, k, :, 1], ALU.add).then_inc(gn[k], 1)

            def norm_var(k, n):
                c0 = ST0 + 8 * k
                dve.wait_ge(gn_pe[k], upto(2, n, 2, IMAGES - 1))
                v_.tensor_scalar(gve[:, k, :], psS[:, 0, c0 + 4:c0 + 6], EPS, None, ALU.add).then_inc(gn[k], 1)

            def norm_finish(k, n):
                dve.wait_ge(gn_pow[k], upto(1, n, 1, IMAGES - 1))
                if k == 0:
                    dve.wait_ge(normed, upto(2, gidx(n - 1, STRIPS - 1), 2))
                    v_.scalar_tensor_tensor(out=nb1[:, :], in0=gme[:, 0, :], scalar=-1.0,
                                                 in1=rs[:, 0, :], op0=ALU.mult, op1=ALU.mult).then_inc(gn[k], 1)
                else:
                    dve.wait_ge(conv_m, upto(9, gidx(n - 1, STRIPS - 1), 9))
                    dve.wait_ge(prods, upto(9, gidx(n - 1, STRIPS - 1), 9))
                    v_.tensor_tensor(mfill[:, :], gme[:, 1, :], bp[:, :], ALU.subtract).then_inc(gn[k], 1)
                    v_.tensor_tensor(weff[:, :, :], cw[:, :, :],
                                          rs[:, 1, :].unsqueeze(2).to_broadcast([128, 2, 9]), ALU.mult).then_inc(gn[k], 1)
                    dve.wait_ge(gn[k], upto(GN_DVE[k], n, 11, IMAGES - 1))
                    v_.tensor_scalar(weff[:, :, 4], weff[:, :, 4], 1.0, None, ALU.add).then_inc(gn[k], 1)
                    v_.tensor_tensor(ms[:, :], mfill[:, :], rs[:, 1, :], ALU.mult).then_inc(gn[k], 1)
                    dve.wait_ge(gn[k], upto(GN_DVE[k], n, 13, IMAGES - 1))
                    v_.tensor_tensor(mw[:, :], ms[:, :], wsum[:, :], ALU.mult).then_inc(gn[k], 1)
                    dve.wait_ge(gn[k], upto(GN_DVE[k], n, 14, IMAGES - 1))
                    v_.tensor_tensor(b2[:, :], bpc[:, :], mw[:, :], ALU.subtract).then_inc(gn[k], 1)

            def pads(n):
                def fill(dst, rows, cols, tl, p0=0):
                    z = zeros[p0:128, 0:rows * cols].rearrange("p (r c) -> p r c", c=cols)
                    v_.tensor_scalar(dst, z, mfill[p0:128, tl:tl + 1], None, ALU.add).then_inc(fixed, 1)

                dve.wait_ge(gn[1], upto(GN_DVE[1], n, 10, IMAGES - 1))
                R, C = MAIN_ROWS, TAIL_ROWS
                v_.tensor_copy(x1main(n, 1, R - 2, 1, 3), x1main(n, 1, R - 2, 57, 3)).then_inc(fixed, 1)
                v_.tensor_copy(x1tail(n, 0, 128, 1, C - 2, 1, 3), x1tail(n, 0, 128, 1, C - 2, 57, 3)).then_inc(fixed, 1)
                dve.wait_ge(fixed, upto(FIX, n, 2, IMAGES - 1))
                fill(x1main(n, 0, R, 0, XW)[:, :, 0:58:57], R, 2, 0)
                fill(x1tail(n, 0, 128, 0, C, 0, XW)[:, :, 0:58:57], C, 2, 1)
                dve.wait_ge(fixed, upto(FIX, n, 4, IMAGES - 1))
                fill(x1main(n, 54, 1, 0, XW), 1, XW, 0)
                fill(x1tail(n, 64, 128, 26, 1, 0, XW), 1, XW, 1, 64)
                dve.wait_ge(fixed, upto(FIX, n, 6, IMAGES - 1))
                v_.tensor_copy(x1main(n, 0, 1, 0, XW), x1main(n, R - 2, 1, 0, XW)).then_inc(fixed, 1)
                v_.tensor_copy(x1main(n, R - 1, 1, 0, XW), x1main(n, 1, 1, 0, XW)).then_inc(fixed, 1)
                v_.tensor_copy(x1tail(n, 0, 64, 0, 1, 0, XW), x1tail(n, 64, 128, 29, 1, 0, XW)).then_inc(fixed, 1)
                v_.tensor_copy(x1tail(n, 0, 64, 29, 1, 0, XW), x1tail(n, 64, 128, 1, 1, 0, XW)).then_inc(fixed, 1)
                v_.tensor_copy(x1tail(n, 64, 128, 0, 1, 0, XW), x1tail(n, 0, 64, 28, 1, 0, XW)).then_inc(fixed, 1)
                v_.tensor_copy(x1tail(n, 64, 128, 30, 1, 0, XW), x1tail(n, 0, 64, 1, 1, 0, XW)).then_inc(fixed, 1)

            def convolve(n, r, i):
                g = gidx(n, r)
                rows = WS + (r == STRIPS - 1)
                y = ym[:, r % 2, 0:rows * WW].rearrange("p (a b) -> p a b", b=WW)
                tap = TAPS[i]
                v = x1main(n, WS * r + tap // 3, rows, tap % 3, WW)
                if i == 0:
                    dve.wait_ge(gn[1], upto(GN_DVE[1], n, GN_DVE[1], IMAGES - 1))
                    dve.wait_ge(fixed, upto(FIX, n, FIX, IMAGES - 1))
                    if not isinstance(n, int) or g >= 2:
                        dve.wait_ge(stored[r % 2], g * 8 - 8 * (r % 2))
                    v_.tensor_scalar(y, v, weff[:, 0, tap:tap + 1], b2[:, 0:1],
                                     ALU.mult, ALU.add).then_inc(conv_m, 1)
                else:
                    dve.wait_ge(conv_m, upto(9, g, i))
                    v_.scalar_tensor_tensor(out=y, in0=v, scalar=weff[:, 0, tap:tap + 1], in1=y,
                                            op0=ALU.mult, op1=ALU.add).then_inc(conv_m, 1)

            def slot(n, r):
                s, o, b, p = stage(n, r, LAG_SCORES), stage(n, r, LAG_OUT), (n, r), stage(n, r, LAG_PROJ)
                a, a1, p1 = stage(n, r, LAG_STATS), stage(n, r, LAG_STATS + 1), stage(n, r, LAG_PROJ + 1)
                c = stage(n, r, LAG_CONV)

                def tap(*which):
                    if live(*c):
                        for i in which:
                            convolve(*c, i)

                if live(*b):
                    low_tail(*b)
                if live(*s):
                    add_bias(*s, 0)
                if closes(*p1):
                    norm_var(1, p1[0])
                if live(*p):
                    residual(*p)
                    dve.wait_ge(resid, upto(4, gidx(*p), 4))
                    if p[1] == 0:
                        dve.wait_ge(gn[1], upto(GN_DVE[1], p[0] - 1, 3, IMAGES - 1))
                if live(*s):
                    maxima(*s, 0)
                if closes(*a1):
                    norm_mean(0, a1[0])
                if closes(*p1):
                    norm_finish(1, p1[0])
                    pads(p1[0])
                tap(0)
                if live(*p):
                    x1_statistics(*p)
                if closes(*p):
                    norm_gather(1, p[0])
                tap(1, 2)
                if live(*s):
                    sums(*s, 0)
                tap(3)
                if live(*s):
                    reciprocals(*s, 0)
                    add_bias(*s, 1)
                if closes(*a1):
                    norm_var(0, a1[0])
                tap(4)
                if live(*s):
                    maxima(*s, 1)
                if closes(*p):
                    norm_mean(1, p[0])
                tap(5)
                if live(*a):
                    x_statistics(*a)
                if closes(*a):
                    norm_gather(0, a[0])
                tap(6)
                if live(*o):
                    o_lows(*o)
                tap(7)
                if live(*s):
                    sums(*s, 1)
                tap(8)
                if live(*s):
                    reciprocals(*s, 1)
                if closes(*a1):
                    norm_finish(0, a1[0])

            schedule(dve, slot)


_SHAPES = [(IMAGES, 128, MAIN_ROWS * WW - 2 * WW), (IMAGES, 128, (TAIL_ROWS - 2) * WW)]


def kernel(x, L0_conv_qkv_w, L0_conv_qkv_b, L0_conv_proj_w, L0_conv_proj_b, L0_conv_rel_table,
           L1_conv_w, L1_conv_b):
    import numpy as _np
    import concourse.bacc as _bacc
    from concourse import mybir as _mybir
    from concourse.bass_utils import run_bass_kernel_spmd as _run

    f = _np.float32
    xs = _np.roll(_np.asarray(x), (-SHIFT, -SHIFT), axis=(1, 2))
    xw = _np.ascontiguousarray(xs.reshape(IMAGES, STRIPS, WS, WIN, WS, CH).transpose(0, 5, 1, 3, 2, 4)
                               ).reshape(IMAGES, CH, PIX)
    order = _np.concatenate([_np.arange(0, 128), CH + _np.arange(0, 128), _np.arange(128, CH),
                             CH + _np.arange(128, CH), 2 * CH + _np.arange(CH)])
    pw = _np.asarray(L0_conv_proj_w)
    wqkv = _np.concatenate([_np.asarray(L0_conv_qkv_w)[:, order], pw, pw[:, 128:]], axis=1)

    def tiles(v, twice=True):
        v = _np.asarray(v)
        return _np.stack([v[:128], _np.concatenate([v[128:], v[128:]])], axis=1)

    qb = _np.asarray(L0_conv_qkv_b)
    vecs = _np.concatenate([tiles(qb[:CH]), tiles(qb[CH:2 * CH]), tiles(qb[2 * CH:]),
                            tiles(L0_conv_proj_b), tiles(L1_conv_b), _np.zeros((128, 2), f)], axis=1)
    cw = _np.asarray(L1_conv_w).reshape(9, CH)
    convw = _np.stack([tiles(cw[t]) for t in range(9)], axis=2)
    co = _np.stack(_np.meshgrid(_np.arange(WS), _np.arange(WS), indexing="ij")).reshape(2, -1)
    rel = (co[:, :, None] - co[:, None, :]) + WS - 1
    idx = rel[0] * (2 * WS - 1) + rel[1]
    tab = _np.asarray(L0_conv_rel_table)[idx].transpose(0, 2, 1)
    bias = _np.zeros((128, HEADS, L), f)
    bias[0:L] = tab
    bias[64:64 + L] = tab
    late = (_np.arange(WS) >= WS - SHIFT).astype(int)
    mask = _np.zeros((128, 2, 2, L), f)
    for row in range(2):
        for col in range(2):
            for w in range(2):
                region = (late[:, None] * 2 * row + late[None, :] * (col and w)).reshape(-1)
                mask[64 * w:64 * w + L, row, col] = _np.where(region[:, None] != region[None, :], -100.0, 0.0)
    grp = _np.arange(CH) // GROUP
    same = (grp[:, None] == grp[None, :]).astype(f) / f(GROUP)
    same = _np.concatenate([same, same[:, 128:]], axis=1)
    gavg = _np.zeros((128, 2, 256), f)
    gavg[:, 0] = same[:128]
    gavg[:64, 1] = same[128:] / 2
    gavg[64:, 1] = same[128:] / 2
    ident = _np.eye(128, dtype=f)

    nc = _bacc.Bacc("TRN2", target_bir_lowering=False, num_devices=1)
    arrays, args = {}, []
    for name, a in (("x", xw), ("wqkv", wqkv), ("vecs", vecs), ("bias", bias), ("mask", mask),
                    ("gavg", gavg), ("convw", convw), ("ident", ident)):
        a = _np.ascontiguousarray(a)
        arrays[f"in_{name}"] = a
        args.append(nc.dram_tensor(f"in_{name}", a.shape, _mybir.dt.from_np(a.dtype), kind="ExternalInput").ap())
    for i, shape in enumerate(_SHAPES):
        args.append(nc.dram_tensor(f"out_{i}", shape, _mybir.dt.float32, kind="ExternalOutput").ap())
    swin_conv_kernel(nc, *args)
    r = _run(nc, [arrays], core_ids=[0])
    ym, yt = r.results[0]["out_0"], r.results[0]["out_1"]
    ym = _np.asarray(ym).reshape(IMAGES, 128, 57, WW)
    yt = _np.asarray(yt).reshape(IMAGES, 2, TAIL, 29, WW)
    main = _np.concatenate([ym[:, :, 54:], ym[:, :, :53]], axis=2)
    tail = _np.concatenate([yt[:, 1, :, 26:], yt[:, 0, :, :28], yt[:, 1, :, :25]], axis=2)
    y = _np.concatenate([main, tail], axis=1).transpose(0, 2, 3, 1)
    return _np.ascontiguousarray(y)
```
